# Optimizing a Trainium2 kernel written in Bass

```python
import numpy as np
import jax
import jax.numpy as jnp

def _softmax(x, axis=-1):
    return jax.nn.softmax(x, axis=axis)

def _gelu(x):
    return jax.nn.gelu(x, approximate=True)

def _silu(x):
    return jax.nn.silu(x)

def _sigmoid(x):
    return jax.nn.sigmoid(x)

def _layernorm(x, axis=-1, eps=1e-05):
    m = jnp.mean(x, axis=axis, keepdims=True)
    v = jnp.var(x, axis=axis, keepdims=True)
    return (x - m) / jnp.sqrt(v + eps)

def _scatter_add(tgt, idx, src, axis=0):
    return tgt.at[idx].add(src)

def _segment_sum(src, seg, n):
    return jax.ops.segment_sum(src, seg, n)
kernel_name = 'mk_decoder_postln_d2_seqx_r4_ed4136'

def setup_inputs(seed: int=0):
    np.random.seed(seed)
    _w = jnp.asarray

    def _rec_inputs():
        import jax
        import jax.numpy as jnp
        _rk = jax.random.key(seed)
        x = -0.0002928 + 1 * jax.random.normal(jax.random.fold_in(_rk, 1), (16, 256, 256), jnp.float32)
        _lenS = 256 - jax.random.randint(jax.random.fold_in(_rk, 7), (16,), 0, max(1, 256 // 4) + 1, jnp.int32)
        _lenS2 = 256 - jax.random.randint(jax.random.fold_in(_rk, 8), (16,), 0, max(1, 256 // 4) + 1, jnp.int32)
        _ctx_1024P = jax.random.normal(jax.random.fold_in(_rk, 11), (16, 16, 256), jnp.float32)
        _ctx_1024c = jax.random.dirichlet(jax.random.fold_in(_rk, 511), 0.3 * jnp.ones((16,), jnp.float32), (16, 256))
        _ctx_1024t = jnp.einsum('bsk,bkd->bsd', _ctx_1024c, _ctx_1024P)
        _ctx_1024t = _ctx_1024t * jax.lax.rsqrt(jnp.mean(jnp.square(_ctx_1024t)) + 1e-12) * 0.953939
        ctx_1024 = -1.39393e-06 + 0.999914 * (_ctx_1024t + 0.3 * jax.random.normal(jax.random.fold_in(_rk, 611), (16, 256, 256), jnp.float32))
        return (x, ctx_1024)
    x, ctx_1024 = _rec_inputs()

    def _L0_attn_setup():
        import jax, jax.numpy as jnp
        import numpy as np
        import math
        B, S, H = (4, 256, 256)
        NQ, NKV = (16, 8)
        HD = H // NQ
        G = HD * NKV
        DEPTH = 1
        LAMBDA_INIT = 0.8 - 0.6 * math.exp(-0.3 * DEPTH)
        key = jax.random.key(seed)
        ks = jax.random.split(key, 7)
        x = jax.random.normal(ks[0], (B, S, H), jnp.float32)
        Wqkv = jax.random.normal(ks[1], (H, 2 * H + 2 * G), jnp.float32) / math.sqrt(H)
        Wproj = jax.random.normal(ks[2], (H, H), jnp.float32) / math.sqrt(H)
        lambda_q1 = 0.1 * jax.random.normal(ks[3], (G,), jnp.float32)
        lambda_k1 = 0.1 * jax.random.normal(ks[4], (G,), jnp.float32)
        lambda_q2 = 0.1 * jax.random.normal(ks[5], (G,), jnp.float32)
        lambda_k2 = 0.1 * jax.random.normal(ks[6], (G,), jnp.float32)
        return {'x': x, 'Wqkv': Wqkv, 'Wproj': Wproj, 'lambda_q1': lambda_q1, 'lambda_k1': lambda_k1, 'lambda_q2': lambda_q2, 'lambda_k2': lambda_k2}
    _L0_attn_all = _L0_attn_setup()
    _L0_attn_in = {k: v for k, v in _L0_attn_all.items() if k in ('Wqkv', 'Wproj', 'lambda_q1', 'lambda_k1', 'lambda_q2', 'lambda_k2')}
    del _L0_attn_all

    def _L0_xattn_setup():
        import jax, jax.numpy as jnp
        import numpy as np
        D_MODEL = 256
        NUM_HEADS = 16
        D_K = D_MODEL // NUM_HEADS
        key = jax.random.key(seed)
        ks = jax.random.split(key, 8)
        B, S = (2, 512)
        query = jax.random.normal(ks[0], (B, S, D_MODEL), dtype=jnp.float32)
        key_t = jax.random.normal(ks[1], (B, S, D_MODEL), dtype=jnp.float32)
        value = jax.random.normal(ks[2], (B, S, D_MODEL), dtype=jnp.float32)
        lim = float(np.sqrt(6.0 / (D_MODEL + D_MODEL)))
        w_q = jax.random.uniform(ks[3], (D_MODEL, D_MODEL), jnp.float32, -lim, lim)
        w_k = jax.random.uniform(ks[4], (D_MODEL, D_MODEL), jnp.float32, -lim, lim)
        w_v = jax.random.uniform(ks[5], (D_MODEL, D_MODEL), jnp.float32, -lim, lim)
        w_o = jax.random.uniform(ks[6], (D_MODEL, D_MODEL), jnp.float32, -lim, lim)
        b_o = jnp.zeros((D_MODEL,), jnp.float32)
        return {'query': query, 'key': key_t, 'value': value, 'w_q': w_q, 'w_k': w_k, 'w_v': w_v, 'w_o': w_o, 'b_o': b_o}
    _L0_xattn_all = _L0_xattn_setup()
    _L0_xattn_in = {k: v for k, v in _L0_xattn_all.items() if k in ('w_q', 'w_k', 'w_v', 'w_o', 'b_o')}
    del _L0_xattn_all

    def _L0_ffn_setup():
        import jax, jax.numpy as jnp
        import numpy as np
        H = 256
        I = 512
        E = 8
        TOP_K = 2
        NUM_SHARED = 1
        key = jax.random.key(seed)
        ks = jax.random.split(key, 9)
        s = 0.02
        x = jax.random.normal(ks[0], (2, 512, H), dtype=jnp.float32)
        sg_w = jax.random.normal(ks[1], (I, H), dtype=jnp.float32) * s
        su_w = jax.random.normal(ks[2], (I, H), dtype=jnp.float32) * s
        sd_w = jax.random.normal(ks[3], (H, I), dtype=jnp.float32) * s
        router_w = jax.random.normal(ks[4], (E, H), dtype=jnp.float32) * s
        routing_bias = jnp.zeros((E,), dtype=jnp.float32)
        wg = jax.random.normal(ks[5], (E, I, H), dtype=jnp.float32) * s
        wu = jax.random.normal(ks[6], (E, I, H), dtype=jnp.float32) * s
        wd = jax.random.normal(ks[7], (E, H, I), dtype=jnp.float32) * s
        return {'x': x, 'sg_w': sg_w, 'su_w': su_w, 'sd_w': sd_w, 'router_w': router_w, 'routing_bias': routing_bias, 'wg': wg, 'wu': wu, 'wd': wd}
    _L0_ffn_all = _L0_ffn_setup()
    _L0_ffn_in = {k: v for k, v in _L0_ffn_all.items() if k in ('sg_w', 'su_w', 'sd_w', 'router_w', 'routing_bias', 'wg', 'wu', 'wd')}
    del _L0_ffn_all

    def _L1_attn_setup():
        import jax, jax.numpy as jnp
        import numpy as np
        from jax import lax
        D_MODEL = 256
        D_STATE = 128
        D_CONV = 4
        EXPAND = 2
        HEADDIM = 64
        D_INNER = EXPAND * D_MODEL
        NHEADS = D_INNER // HEADDIM
        CONV_DIM = D_INNER + 2 * D_STATE
        D_IN_PROJ = 2 * D_INNER + 2 * D_STATE + NHEADS
        EPS = 1e-05

        def _ssm_forward(x, in_proj_w, conv_w, conv_b, norm_w, out_proj_w, dt_bias, A_log, D_param):
            B, L, _ = x.shape
            zxbcdt = jnp.einsum('bld,ed->ble', x, in_proj_w)
            z = zxbcdt[..., :D_INNER]
            xBC = zxbcdt[..., D_INNER:D_INNER + CONV_DIM]
            dt = zxbcdt[..., D_INNER + CONV_DIM:]
            xBC_c = lax.conv_general_dilated(xBC.transpose(0, 2, 1), conv_w, window_strides=(1,), padding=[(D_CONV - 1, 0)], feature_group_count=CONV_DIM, dimension_numbers=('NCH', 'OIH', 'NCH'))
            xBC = jax.nn.silu((xBC_c + conv_b[None, :, None]).transpose(0, 2, 1))
            x_part = xBC[..., :D_INNER]
            B_part = xBC[..., D_INNER:D_INNER + D_STATE]
            C_part = xBC[..., D_INNER + D_STATE:]
            x_heads = x_part.reshape(B, L, NHEADS, HEADDIM)
            dt = jax.nn.softplus(dt + dt_bias)
            A = -jnp.exp(A_log)

            def step(state, inp):
                x_t, B_t, C_t, dt_t = inp
                decay = jnp.exp(A[None, :] * dt_t)
                state = state * decay[:, :, None, None] + (x_t * dt_t[:, :, None])[..., None] * B_t[:, None, None, :]
                y_t = jnp.einsum('bhpn,bn->bhp', state, C_t)
                return (state, y_t)
            state0 = jnp.zeros((B, NHEADS, HEADDIM, D_STATE), dtype=x.dtype)
            inputs = (jnp.moveaxis(x_heads, 1, 0), jnp.moveaxis(B_part, 1, 0), jnp.moveaxis(C_part, 1, 0), jnp.moveaxis(dt, 1, 0))
            _, y_seq = lax.scan(step, state0, inputs)
            y = jnp.moveaxis(y_seq, 0, 1).reshape(B, L, D_INNER)
            D_full = jnp.repeat(D_param, HEADDIM)
            y = y + x_part * D_full
            y = y * jax.nn.silu(z)
            y = y * jax.lax.rsqrt(jnp.mean(y * y, axis=-1, keepdims=True) + EPS) * norm_w
            return jnp.einsum('ble,de->bld', y, out_proj_w)
        key = jax.random.key(seed)
        ks = jax.random.split(key, 8)
        B, L = (2, 512)
        x = jax.random.normal(ks[0], (B, L, D_MODEL), dtype=jnp.float32)
        in_proj_w = jax.random.normal(ks[1], (D_IN_PROJ, D_MODEL), dtype=jnp.float32) * 0.02
        conv_w = jax.random.normal(ks[2], (CONV_DIM, 1, D_CONV), dtype=jnp.float32) * 0.2
        conv_b = jax.random.normal(ks[3], (CONV_DIM,), dtype=jnp.float32) * 0.02
        norm_w = jnp.ones((D_INNER,), dtype=jnp.float32)
        out_proj_w = jax.random.normal(ks[4], (D_MODEL, D_INNER), dtype=jnp.float32) * 0.02
        dt_bias = jax.random.normal(ks[5], (NHEADS,), dtype=jnp.float32) * 0.1
        A_log = jax.random.normal(ks[6], (NHEADS,), dtype=jnp.float32) * 0.1
        D_param = jnp.ones((NHEADS,), dtype=jnp.float32)
        return {'x': x, 'in_proj_w': in_proj_w, 'conv_w': conv_w, 'conv_b': conv_b, 'norm_w': norm_w, 'out_proj_w': out_proj_w, 'dt_bias': dt_bias, 'A_log': A_log, 'D_param': D_param}
    _L1_attn_all = _L1_attn_setup()
    _L1_attn_in = {k: v for k, v in _L1_attn_all.items() if k in ('in_proj_w', 'conv_w', 'conv_b', 'norm_w', 'out_proj_w', 'dt_bias', 'A_log', 'D_param')}
    del _L1_attn_all

    def _L1_xattn_setup():
        import jax, jax.numpy as jnp
        import numpy as np
        import math
        D_MODEL = 256
        N_HEADS = 16
        key = jax.random.key(seed)
        ks = jax.random.split(key, 11)
        N, L, S = (2, 512, 512)
        d = D_MODEL
        s = 1.0 / math.sqrt(d)
        return {'queries': jax.random.normal(ks[0], (N, L, d), dtype=jnp.float32), 'keys': jax.random.normal(ks[1], (N, S, d), dtype=jnp.float32), 'values': jax.random.normal(ks[2], (N, S, d), dtype=jnp.float32), 'Wq': jax.random.normal(ks[3], (d, d), dtype=jnp.float32) * s, 'bq': jax.random.normal(ks[4], (d,), dtype=jnp.float32) * s, 'Wk': jax.random.normal(ks[5], (d, d), dtype=jnp.float32) * s, 'bk': jax.random.normal(ks[6], (d,), dtype=jnp.float32) * s, 'Wv': jax.random.normal(ks[7], (d, d), dtype=jnp.float32) * s, 'bv': jax.random.normal(ks[8], (d,), dtype=jnp.float32) * s, 'Wo': jax.random.normal(ks[9], (d, d), dtype=jnp.float32) * s, 'bo': jax.random.normal(ks[10], (d,), dtype=jnp.float32) * s}
    _L1_xattn_all = _L1_xattn_setup()
    _L1_xattn_in = {k: v for k, v in _L1_xattn_all.items() if k in ('Wq', 'bq', 'Wk', 'bk', 'Wv', 'bv', 'Wo', 'bo')}
    del _L1_xattn_all

    def _L1_ffn_setup():
        import jax, jax.numpy as jnp
        import numpy as np
        D_MODEL, D_FF, NUM_EXPERTS, RANK, TOP_K = (256, 1024, 8, 16, 2)
        B, S = (8, 512)

        def _expert_ffn(h, wi_w, wo_w, A, Bm):
            inter = jnp.einsum('bsd,fd->bsf', h, wi_w)
            lora = jnp.einsum('bsr,fr->bsf', jnp.einsum('bsd,rd->bsr', h, A), Bm)
            inter = jax.nn.relu(inter + lora)
            return jnp.einsum('bsf,df->bsd', inter, wo_w)
        key = jax.random.key(seed)
        ks = jax.random.split(key, 8)
        hidden_states = jax.random.normal(ks[0], (B, S, D_MODEL), dtype=jnp.float32)
        wi_w = jax.random.normal(ks[1], (D_FF, D_MODEL), dtype=jnp.float32) * (1.0 / np.sqrt(D_MODEL))
        wo_w = jax.random.normal(ks[2], (D_MODEL, D_FF), dtype=jnp.float32) * (1.0 / np.sqrt(D_FF))
        lora_As = jax.random.uniform(ks[3], (NUM_EXPERTS, RANK, D_MODEL), dtype=jnp.float32, minval=-1.0, maxval=1.0) / np.sqrt(D_MODEL)
        lora_Bs = jax.random.normal(ks[4], (NUM_EXPERTS, D_FF, RANK), dtype=jnp.float32) * 0.02
        top_k_indices = jnp.arange(TOP_K, dtype=jnp.int32)
        top_k_values = jax.random.uniform(ks[5], (TOP_K,), dtype=jnp.float32)
        return {'hidden_states': hidden_states, 'wi_w': wi_w, 'wo_w': wo_w, 'lora_As': lora_As, 'lora_Bs': lora_Bs, 'top_k_indices': top_k_indices, 'top_k_values': top_k_values}
    _L1_ffn_all = _L1_ffn_setup()
    _L1_ffn_in = {k: v for k, v in _L1_ffn_all.items() if k in ('wi_w', 'wo_w', 'lora_As', 'lora_Bs', 'top_k_indices', 'top_k_values')}
    del _L1_ffn_all
    return {'x': x, 'ctx_1024': ctx_1024, 'L0_attn_Wqkv': _L0_attn_in['Wqkv'], 'L0_attn_Wproj': _L0_attn_in['Wproj'], 'L0_attn_lambda_q1': _L0_attn_in['lambda_q1'], 'L0_attn_lambda_k1': _L0_attn_in['lambda_k1'], 'L0_attn_lambda_q2': _L0_attn_in['lambda_q2'], 'L0_attn_lambda_k2': _L0_attn_in['lambda_k2'], 'L0_xattn_w_q': _L0_xattn_in['w_q'], 'L0_xattn_w_k': _L0_xattn_in['w_k'], 'L0_xattn_w_v': _L0_xattn_in['w_v'], 'L0_xattn_w_o': _L0_xattn_in['w_o'], 'L0_xattn_b_o': _L0_xattn_in['b_o'], 'L0_ffn_sg_w': _L0_ffn_in['sg_w'], 'L0_ffn_su_w': _L0_ffn_in['su_w'], 'L0_ffn_sd_w': _L0_ffn_in['sd_w'], 'L0_ffn_router_w': _L0_ffn_in['router_w'], 'L0_ffn_routing_bias': _L0_ffn_in['routing_bias'], 'L0_ffn_wg': _L0_ffn_in['wg'], 'L0_ffn_wu': _L0_ffn_in['wu'], 'L0_ffn_wd': _L0_ffn_in['wd'], 'L1_attn_in_proj_w': _L1_attn_in['in_proj_w'], 'L1_attn_conv_w': _L1_attn_in['conv_w'], 'L1_attn_conv_b': _L1_attn_in['conv_b'], 'L1_attn_norm_w': _L1_attn_in['norm_w'], 'L1_attn_out_proj_w': _L1_attn_in['out_proj_w'], 'L1_attn_dt_bias': _L1_attn_in['dt_bias'], 'L1_attn_A_log': _L1_attn_in['A_log'], 'L1_attn_D_param': _L1_attn_in['D_param'], 'L1_xattn_Wq': _L1_xattn_in['Wq'], 'L1_xattn_bq': _L1_xattn_in['bq'], 'L1_xattn_Wk': _L1_xattn_in['Wk'], 'L1_xattn_bk': _L1_xattn_in['bk'], 'L1_xattn_Wv': _L1_xattn_in['Wv'], 'L1_xattn_bv': _L1_xattn_in['bv'], 'L1_xattn_Wo': _L1_xattn_in['Wo'], 'L1_xattn_bo': _L1_xattn_in['bo'], 'L1_ffn_wi_w': _L1_ffn_in['wi_w'], 'L1_ffn_wo_w': _L1_ffn_in['wo_w'], 'L1_ffn_lora_As': _L1_ffn_in['lora_As'], 'L1_ffn_lora_Bs': _L1_ffn_in['lora_Bs'], 'L1_ffn_top_k_indices': _L1_ffn_in['top_k_indices'], 'L1_ffn_top_k_values': _L1_ffn_in['top_k_values']}

def reference(x, ctx_1024, L0_attn_Wqkv, L0_attn_Wproj, L0_attn_lambda_q1, L0_attn_lambda_k1, L0_attn_lambda_q2, L0_attn_lambda_k2, L0_xattn_w_q, L0_xattn_w_k, L0_xattn_w_v, L0_xattn_w_o, L0_xattn_b_o, L0_ffn_sg_w, L0_ffn_su_w, L0_ffn_sd_w, L0_ffn_router_w, L0_ffn_routing_bias, L0_ffn_wg, L0_ffn_wu, L0_ffn_wd, L1_attn_in_proj_w, L1_attn_conv_w, L1_attn_conv_b, L1_attn_norm_w, L1_attn_out_proj_w, L1_attn_dt_bias, L1_attn_A_log, L1_attn_D_param, L1_xattn_Wq, L1_xattn_bq, L1_xattn_Wk, L1_xattn_bk, L1_xattn_Wv, L1_xattn_bv, L1_xattn_Wo, L1_xattn_bo, L1_ffn_wi_w, L1_ffn_wo_w, L1_ffn_lora_As, L1_ffn_lora_Bs, L1_ffn_top_k_indices, L1_ffn_top_k_values):
    import jax
    import jax.numpy as jnp

    def _L0_attn_ref(x, Wqkv, Wproj, lambda_q1, lambda_k1, lambda_q2, lambda_k2):
        import jax, jax.numpy as jnp
        import numpy as np
        import math
        B, S, H = (4, 256, 256)
        NQ, NKV = (16, 8)
        HD = H // NQ
        G = HD * NKV
        DEPTH = 1
        LAMBDA_INIT = 0.8 - 0.6 * math.exp(-0.3 * DEPTH)
        Bx, Sx, Hx = x.shape
        qkv = x @ Wqkv
        q = qkv[..., :2 * Hx].reshape(Bx, 2 * NQ, Sx, HD)
        k = qkv[..., 2 * Hx:2 * Hx + G].reshape(Bx, NKV, Sx, HD)
        v = qkv[..., 2 * Hx + G:].reshape(Bx, NKV, Sx, HD)
        k = jnp.repeat(k, 2 * NQ // NKV, axis=1)
        v = jnp.repeat(v, NQ // NKV, axis=1)
        scores = jnp.einsum('bhqd,bhkd->bhqk', q, k) / math.sqrt(HD)
        causal = jnp.tril(jnp.ones((Sx, Sx), dtype=bool))
        scores = jnp.where(causal, scores, -jnp.inf)
        aw = jax.nn.softmax(scores, axis=-1)
        lam1 = jnp.exp(jnp.sum(lambda_q1 * lambda_k1))
        lam2 = jnp.exp(jnp.sum(lambda_q2 * lambda_k2))
        lam = lam1 - lam2 + LAMBDA_INIT
        aw = aw.reshape(Bx, NQ, 2, Sx, Sx)
        aw = aw[:, :, 0] - lam * aw[:, :, 1]
        attn = jnp.einsum('bhqk,bhkd->bhqd', aw, v) * (1.0 - LAMBDA_INIT)
        attn = jnp.transpose(attn, (0, 2, 1, 3)).reshape(Bx, Sx, Hx)
        y = attn @ Wproj
        y = jnp.transpose(y, (0, 2, 1)).reshape(Bx, Sx, Hx)
        return y @ Wproj

    def _L0_xattn_ref(query, key, value, w_q, w_k, w_v, w_o, b_o):
        import jax, jax.numpy as jnp
        import numpy as np
        D_MODEL = 256
        NUM_HEADS = 16
        D_K = D_MODEL // NUM_HEADS
        B, S, _ = query.shape
        H, Dk = (NUM_HEADS, D_K)

        def proj(x, w):
            return (x @ w.T).reshape(B, S, H, Dk).transpose(0, 2, 1, 3)
        Q = proj(query, w_q)
        K = proj(key, w_k)
        V = proj(value, w_v)
        scores = jnp.einsum('bhqd,bhkd->bhqk', Q, K) / jnp.sqrt(jnp.float32(Dk))
        attn = jax.nn.softmax(scores, axis=-1)
        out = jnp.einsum('bhqk,bhkd->bhqd', attn, V)
        out = out.transpose(0, 2, 1, 3).reshape(B, S, H * Dk)
        return out @ w_o.T + b_o

    def _L0_ffn_ref(x, sg_w, su_w, sd_w, router_w, routing_bias, wg, wu, wd):
        import jax, jax.numpy as jnp
        import numpy as np
        H = 256
        I = 512
        E = 8
        TOP_K = 2
        NUM_SHARED = 1
        orig_shape = x.shape
        xt = x.reshape(-1, H)
        T = xt.shape[0]
        shared = jax.nn.silu(xt @ sg_w.T) * (xt @ su_w.T) @ sd_w.T
        shared = shared / NUM_SHARED
        logits = xt @ router_w.T + routing_bias
        probs = jax.nn.sigmoid(logits)
        topk_p, topk_idx = jax.lax.top_k(probs, TOP_K)
        topk_p = topk_p / jnp.sum(topk_p, axis=-1, keepdims=True)
        w = jnp.zeros((T, E), dtype=xt.dtype)
        w = w.at[jnp.arange(T)[:, None], topk_idx].add(topk_p)
        g = jnp.einsum('th,eih->tei', xt, wg)
        u = jnp.einsum('th,eih->tei', xt, wu)
        h = jax.nn.silu(g) * u
        y = jnp.einsum('tei,ehi->teh', h, wd)
        routed = jnp.einsum('te,teh->th', w, y)
        return (shared + routed).reshape(orig_shape)

    def _L1_attn_ref(x, in_proj_w, conv_w, conv_b, norm_w, out_proj_w, dt_bias, A_log, D_param):
        import jax, jax.numpy as jnp
        import numpy as np
        from jax import lax
        D_MODEL = 256
        D_STATE = 128
        D_CONV = 4
        EXPAND = 2
        HEADDIM = 64
        D_INNER = EXPAND * D_MODEL
        NHEADS = D_INNER // HEADDIM
        CONV_DIM = D_INNER + 2 * D_STATE
        D_IN_PROJ = 2 * D_INNER + 2 * D_STATE + NHEADS
        EPS = 1e-05

        def _ssm_forward(x, in_proj_w, conv_w, conv_b, norm_w, out_proj_w, dt_bias, A_log, D_param):
            B, L, _ = x.shape
            zxbcdt = jnp.einsum('bld,ed->ble', x, in_proj_w)
            z = zxbcdt[..., :D_INNER]
            xBC = zxbcdt[..., D_INNER:D_INNER + CONV_DIM]
            dt = zxbcdt[..., D_INNER + CONV_DIM:]
            xBC_c = lax.conv_general_dilated(xBC.transpose(0, 2, 1), conv_w, window_strides=(1,), padding=[(D_CONV - 1, 0)], feature_group_count=CONV_DIM, dimension_numbers=('NCH', 'OIH', 'NCH'))
            xBC = jax.nn.silu((xBC_c + conv_b[None, :, None]).transpose(0, 2, 1))
            x_part = xBC[..., :D_INNER]
            B_part = xBC[..., D_INNER:D_INNER + D_STATE]
            C_part = xBC[..., D_INNER + D_STATE:]
            x_heads = x_part.reshape(B, L, NHEADS, HEADDIM)
            dt = jax.nn.softplus(dt + dt_bias)
            A = -jnp.exp(A_log)

            def step(state, inp):
                x_t, B_t, C_t, dt_t = inp
                decay = jnp.exp(A[None, :] * dt_t)
                state = state * decay[:, :, None, None] + (x_t * dt_t[:, :, None])[..., None] * B_t[:, None, None, :]
                y_t = jnp.einsum('bhpn,bn->bhp', state, C_t)
                return (state, y_t)
            state0 = jnp.zeros((B, NHEADS, HEADDIM, D_STATE), dtype=x.dtype)
            inputs = (jnp.moveaxis(x_heads, 1, 0), jnp.moveaxis(B_part, 1, 0), jnp.moveaxis(C_part, 1, 0), jnp.moveaxis(dt, 1, 0))
            _, y_seq = lax.scan(step, state0, inputs)
            y = jnp.moveaxis(y_seq, 0, 1).reshape(B, L, D_INNER)
            D_full = jnp.repeat(D_param, HEADDIM)
            y = y + x_part * D_full
            y = y * jax.nn.silu(z)
            y = y * jax.lax.rsqrt(jnp.mean(y * y, axis=-1, keepdims=True) + EPS) * norm_w
            return jnp.einsum('ble,de->bld', y, out_proj_w)
        return _ssm_forward(x, in_proj_w, conv_w, conv_b, norm_w, out_proj_w, dt_bias, A_log, D_param)

    def _L1_xattn_ref(queries, keys, values, Wq, bq, Wk, bk, Wv, bv, Wo, bo):
        import jax, jax.numpy as jnp
        import numpy as np
        import math
        D_MODEL = 256
        N_HEADS = 16
        N, L, _ = queries.shape
        S = keys.shape[1]
        H = N_HEADS
        q = (queries @ Wq.T + bq).reshape(N, L, H, -1)
        k = (keys @ Wk.T + bk).reshape(N, S, H, -1)
        v = (values @ Wv.T + bv).reshape(N, S, H, -1)
        D = k.shape[-1]
        sm = jnp.einsum('nlhd,nshd->nlhs', q, k) / math.sqrt(D)
        causal_mask = jnp.triu(jnp.ones((L, S), dtype=bool), k=1)
        sm = jnp.where(causal_mask[None, :, None, :], -jnp.inf, sm)
        sm = jax.nn.softmax(sm, axis=-1)
        attn = jnp.einsum('nlhs,nshd->nlhd', sm, v)
        new_values = attn.reshape(N, L, H * D)
        return new_values @ Wo.T + bo

    def _L1_ffn_ref(hidden_states, wi_w, wo_w, lora_As, lora_Bs, top_k_indices, top_k_values):
        import jax, jax.numpy as jnp
        import numpy as np
        D_MODEL, D_FF, NUM_EXPERTS, RANK, TOP_K = (256, 1024, 8, 16, 2)
        B, S = (8, 512)

        def _expert_ffn(h, wi_w, wo_w, A, Bm):
            inter = jnp.einsum('bsd,fd->bsf', h, wi_w)
            lora = jnp.einsum('bsr,fr->bsf', jnp.einsum('bsd,rd->bsr', h, A), Bm)
            inter = jax.nn.relu(inter + lora)
            return jnp.einsum('bsf,df->bsd', inter, wo_w)
        out = jnp.zeros_like(hidden_states)
        for k in range(top_k_values.shape[0]):
            A = jnp.take(lora_As, top_k_indices[k], axis=0)
            Bm = jnp.take(lora_Bs, top_k_indices[k], axis=0)
            out = out + top_k_values[k] * _expert_ffn(hidden_states, wi_w, wo_w, A, Bm)
        return out
    x = _layernorm(x + _L0_attn_ref(x, L0_attn_Wqkv, L0_attn_Wproj, L0_attn_lambda_q1, L0_attn_lambda_k1, L0_attn_lambda_q2, L0_attn_lambda_k2), axis=-1)
    x = _layernorm(x + _L0_xattn_ref(x, ctx_1024, ctx_1024, L0_xattn_w_q, L0_xattn_w_k, L0_xattn_w_v, L0_xattn_w_o, L0_xattn_b_o), axis=-1)
    x = _layernorm(x + _L0_ffn_ref(x, L0_ffn_sg_w, L0_ffn_su_w, L0_ffn_sd_w, L0_ffn_router_w, L0_ffn_routing_bias, L0_ffn_wg, L0_ffn_wu, L0_ffn_wd), axis=-1)
    x = _layernorm(x + _L1_attn_ref(x, L1_attn_in_proj_w, L1_attn_conv_w, L1_attn_conv_b, L1_attn_norm_w, L1_attn_out_proj_w, L1_attn_dt_bias, L1_attn_A_log, L1_attn_D_param), axis=-1)
    x = _layernorm(x + _L1_xattn_ref(x, ctx_1024, ctx_1024, L1_xattn_Wq, L1_xattn_bq, L1_xattn_Wk, L1_xattn_bk, L1_xattn_Wv, L1_xattn_bv, L1_xattn_Wo, L1_xattn_bo), axis=-1)
    x = _layernorm(x + _L1_ffn_ref(x, L1_ffn_wi_w, L1_ffn_wo_w, L1_ffn_lora_As, L1_ffn_lora_Bs, L1_ffn_top_k_indices, L1_ffn_top_k_values), axis=-1)
    return x

_drawn_inputs = setup_inputs


def setup_inputs(seed=0):
    import zlib

    import numpy as np

    out = dict(_drawn_inputs(seed))
    spreads = {'L0_xattn_b_o': (0.0, 0.1),
     'L0_ffn_routing_bias': (0.0, 0.8),
     'L1_attn_norm_w': (1.0, 0.2),
     'L1_attn_D_param': (1.0, 0.2)}
    factors = {'L0_attn_lambda_q1': 8.0,
     'L0_attn_lambda_k1': 8.0,
     'L0_attn_lambda_q2': 43.296,
     'L0_attn_lambda_k2': 12.696,
     'L0_ffn_router_w': 4.062,
     'L0_ffn_wg': 3.537,
     'L0_ffn_wu': 3.503,
     'L0_ffn_wd': 3.495,
     'L1_attn_dt_bias': 63.458,
     'L1_attn_A_log': 64.0,
     'L1_xattn_bq': 4.3,
     'L1_xattn_bk': 64.0,
     'L1_ffn_top_k_values': 64.0,
     'L0_ffn_sg_w': 2.789,
     'L0_ffn_su_w': 2.943,
     'L0_ffn_sd_w': 2.733}
    for name, (base, spread) in spreads.items():
        noise = np.random.default_rng([zlib.crc32(name.encode()), seed]).standard_normal(out[name].shape)
        drawn = base * np.exp(spread * noise) if base else spread * noise
        out[name] = jnp.asarray(drawn.astype(out[name].dtype))
    for name, factor in factors.items():
        out[name] = (out[name] * factor).astype(out[name].dtype)
    return out
```

```python
import math
from contextlib import ExitStack

import numpy as np

import concourse.bass as bass
import concourse.mybir as mybir
from concourse.alu_op_type import AluOpType as ALU

ACT = mybir.ActivationFunctionType
AX = mybir.AxisListType
F32 = mybir.dt.float32
F32R = mybir.dt.float32r
BF16 = mybir.dt.bfloat16
I32 = mybir.dt.int32
U32 = mybir.dt.uint32

P = 128
B = 16
S = 256
D = 256
QT = S // P
KT = D // P
HD = 16
EPS = 1e-5
LAMBDA_INIT = 0.8 - 0.6 * math.exp(-0.3)
MASKED = -1e30


class Step:

    def __init__(self, j, c, count=B):
        self.j, self.c, self.count = j, c, count

    def at(self, d=0):
        return self.j * 2 + (self.c + d)

    def nth(self, d=0):
        return self.j + (self.c + d) // 2

    def parity(self, d=0):
        return (self.c + d) % 2

    def has(self, d):
        return not isinstance(self.j, int) or 0 <= self.at(d) < self.count

    def done(self, d=0):
        if isinstance(self.j, int):
            return min(max(self.at(d) + 1, 0), self.count)
        return self.at(d) + 1


def batches(eng, body, first, last, peel_head, peel_tail, count=B):
    lo, hi = first + peel_head, last + 1 - peel_tail
    pairs = (hi - lo) // 2
    for t in range(first, lo):
        body(Step(0, t, count))
    with eng.Fori(0, pairs) as j:
        body(Step(j, lo, count))
        body(Step(j, lo + 1, count))
    for t in range(lo + 2 * pairs, last + 1):
        body(Step(0, t, count))


def product3(pe, out, a, b, start, stop, **kw):
    pe.matmul(out, a[0], b[0], start=start, stop=False, **kw)
    pe.matmul(out, a[0], b[1], start=False, stop=False, **kw)
    return pe.matmul(out, a[1], b[0], start=False, stop=stop, **kw)


class Memory:

    def __init__(self, nc, stack, stage):
        self.nc, self.stack, self.stage = nc, stack, stage
        self.numbers = []

    def sb(self, name, shape, dt=F32):
        return self.stack.enter_context(self.nc.sbuf_tensor(f"{self.stage}_{name}", shape, dt))

    def ps(self, name, shape=(P, 512), dt=F32):
        return self.stack.enter_context(self.nc.psum_tensor(f"{self.stage}_{name}", list(shape), dt))

    def sem(self, name):
        semaphore = self.stack.enter_context(self.nc.semaphore(f"{self.stage}_{name}"))
        self.numbers.append(semaphore.num)
        return semaphore

    def sems(self, name, n=2):
        return [self.sem(f"{name}{i}") for i in range(n)]

    def block(self):
        self.stack.callback(self.clear_semaphores)
        return self.stack.enter_context(self.nc.Block())

    def clear_semaphores(self):
        with self.nc.Block() as block:
            @block.gpsimd
            def _(pool):
                first = last = None
                for number in sorted(self.numbers):
                    if first is None or number != last + 1:
                        if first is not None:
                            pool.sem_clear(range(first, last + 1))
                        first = number
                    last = number
                pool.sem_clear(range(first, last + 1))


class RowNorm:

    def __init__(self, m, x_in, x_out, y_done):
        self.m, self.y_done = m, y_done
        self.x_rows = x_in.rearrange("(b q p) d -> b p q d", q=QT, p=P)
        self.o_rows = x_out.rearrange("(b q p) d -> b p q d", q=QT, p=P)
        self.x_res = [m.sb(f"x_res{i}", [P, QT, D]) for i in range(2)]
        self.y_out = [m.sb(f"y_out{i}", [P, QT, D]) for i in range(2)]
        self.r, self.stats, self.mv = m.sb("r", [P, QT, D]), m.sb("stats", [P, QT, 6]), m.sb("mv", [P, QT, 2])
        self.gate, self.var_eps, self.rstd = m.sb("gate", [P, 1]), m.sb("var_eps", [P, QT]), m.sb("rstd", [P, QT])
        self.neg_half = m.sb("neg_half", [P, QT])
        self.half_set = m.sem("half_set")
        self.res_loaded, self.stored = m.sems("res_loaded"), m.sems("stored")
        self.r_ready, self.stat_ready, self.mean_ready, self.eps_ready = (
            m.sem("r_ready"), m.sem("stat_ready"), m.sem("mean_ready"), m.sem("eps_ready"))
        self.rstd_ready, self.out_ready = m.sem("rstd_ready"), m.sem("out_ready")

    def load(self, sp, st, d):
        p = st.parity(d)
        if st.has(d - 2):
            sp.wait_ge(self.r_ready, st.done(d - 2))
        sp.dma_start(self.x_res[p][:], self.x_rows[st.at(d)]).then_inc(self.res_loaded[p], 16)

    def store(self, sp, st, d):
        sp.wait_ge(self.out_ready, st.done(d))
        sp.dma_start(self.o_rows[st.at(d)], self.y_out[st.parity(d)][:]).then_inc(self.stored[st.parity(d)], 16)

    def all_stored(self, sp):
        for p in range(2):
            sp.wait_ge(self.stored[p], B // 2 * 16)

    def residual(self, dve, st, d, banks, row_scale=None):
        n, p = st.done(d), st.parity(d)
        dve.wait_ge(self.y_done, n)
        dve.wait_ge(self.res_loaded[p], (st.nth(d) + 1) * 16)
        if st.has(d - 1):
            dve.wait_ge(self.out_ready, st.done(d - 1))
        for q in range(QT):
            if row_scale is None:
                last = dve.tensor_tensor(self.r[:, q, :], banks[q], self.x_res[p][:, q, :], ALU.add)
            else:
                last = dve.scalar_tensor_tensor(self.r[:, q, :], banks[q], row_scale[:, q:q + 1],
                                                self.x_res[p][:, q, :], ALU.mult, ALU.add)
        last.then_inc(self.r_ready, 1)
        dve.wait_ge(self.r_ready, n)
        for q in range(QT):
            dve.bn_stats(self.stats[:, q, :], self.r[:, q, :]).then_inc(self.stat_ready, 1)
        dve.wait_ge(self.stat_ready, 2 * n)
        dve.memset(self.gate[:], 0.0)
        for q in range(QT):
            dve.bn_aggr(self.mv[:, q, :], self.stats[:, q, :]).then_inc(self.mean_ready, 1)
        dve.wait_ge(self.mean_ready, 2 * n)
        dve.tensor_scalar(self.var_eps[:], self.mv[:, :, 1], EPS, None, ALU.add).then_inc(self.eps_ready, 1)

    def constants(self, pool):
        pool.memset(self.neg_half[:], -0.5).then_inc(self.half_set, 1)
        pool.wait_ge(self.half_set, 1)

    def inverse_root(self, pool, st, d):
        pool.wait_ge(self.eps_ready, st.done(d))
        pool.tensor_tensor(self.rstd[:], self.var_eps[:], self.neg_half[:], ALU.pow).then_inc(self.rstd_ready, 1)

    def finish(self, dve, st, d):
        p = st.parity(d)
        dve.wait_ge(self.rstd_ready, st.done(d))
        if st.has(d - 2):
            dve.wait_ge(self.stored[p], st.nth(d) * 16)
        for q in range(QT):
            last = dve.tensor_scalar(self.y_out[p][:, q, :], self.r[:, q, :], self.mv[:, q, 0:1],
                                     self.rstd[:, q:q + 1], ALU.subtract, ALU.mult)
        last.then_inc(self.out_ready, 1)



def cross_attention(nc, stage, x_in, x_out, ctx_t, weights, biases, bias_cols, consts, causal):
    H = 16
    HALF = H // 2
    STK = 4 * HD
    has_qkv_bias = bias_cols is not None
    with ExitStack() as stack:
        m = Memory(nc, stack, stage)
        w_all = m.sb("w_all", [P, 4, KT, D])
        w_hi = m.sb("w_hi", [P, 4, KT, D], F32R)
        w_lo = m.sb("w_lo", [P, 4, KT, D], F32R)
        ident = m.sb("ident", [P, P])
        identb = m.sb("identb", [P, P], BF16)
        mask = m.sb("mask", [P, 2, P], BF16)
        ones = m.sb("ones", [P, 2, 32])
        bvo = m.sb("bvo", [P, 2, D])
        bqk = m.sb("bqk", [P, 4])
        x_tok = [m.sb(f"x_tok{i}", [P, QT, D]) for i in range(2)]
        c_t = [m.sb(f"c_t{i}", [P, KT, S]) for i in range(2)]
        x_hi = m.sb("x_hi", [P, KT, S], F32R)
        x_lo = m.sb("x_lo", [P, KT, S], F32R)
        c_hi = m.sb("c_hi", [P, KT, S], F32R)
        c_lo = m.sb("c_lo", [P, KT, S], F32R)
        q_full = m.sb("q_full", [P, KT, S])
        k_full = m.sb("k_full", [P, KT, S])
        q_split = m.sb("q_split", [P, 2, KT, S], F32R)
        k_split = m.sb("k_split", [P, 2, KT, S], F32R)
        q_stack = [m.sb(f"q_stack{i}", [P, H, S], F32R) for i in range(2)]
        k_stack = [m.sb(f"k_stack{i}", [P, H, S], F32R) for i in range(2)]
        v_full = m.sb("v_full", [P, QT, D])
        v_pad = [m.sb(f"v_pad{i}", [P, QT, H // 2, 2, 2, HD]) for i in range(2)]
        neg_max = [m.sb(f"neg_max{i}", [P, H, QT]) for i in range(2)]
        max_row = m.sb("max_row", [HALF * QT, 2, P], F32R)
        zero_row = m.sb("zero_row", [HALF * QT, P])
        probs = [m.sb(f"probs{i}", [P, 4, 2 * S]) for i in range(2)]
        inv_sum = m.sb("inv_sum", [P, 2, S])
        o_full = m.sb("o_full", [P, 2, S])
        o_hi = m.sb("o_hi", [P, 2, S], F32R)
        o_lo = m.sb("o_lo", [P, 2, S], F32R)
        x_res = [m.sb(f"x_res{i}", [P, QT, D]) for i in range(2)]
        r = m.sb("r", [P, QT, D])
        stats = m.sb("stats", [P, QT, 6])
        gate = m.sb("gate", [P, 1])
        mv = m.sb("mv", [P, QT, 2])
        neg_half = m.sb("neg_half", [P, QT])
        var_eps = m.sb("var_eps", [P, QT])
        rstd = m.sb("rstd", [P, QT])
        y_out = [m.sb(f"y_out{i}", [P, QT, D]) for i in range(2)]

        misc = [m.ps(f"misc{i}") for i in range(2)]
        max_ps = [m.ps(f"max_ps{i}") for i in range(2)]
        score_ps = [m.ps(f"score_ps{i}") for i in range(2)]
        out_ps = [m.ps(f"out_ps{i}") for i in range(2)]

        qk_dram = [nc.dram_tensor(f"{stage}_qk{i}", (2, 2, D, S), F32, kind="Internal").ap()
                   for i in range(2)]

        consts_loaded = m.sem("consts_loaded")
        w_hi_ready, w_lo_ready = m.sem("w_hi_ready"), m.sem("w_lo_ready")
        zeroed, v_zeroed = m.sem("zeroed"), m.sem("v_zeroed")
        x_loaded, c_loaded, res_loaded = m.sems("x_loaded"), m.sems("c_loaded"), m.sems("res_loaded")
        stored = m.sems("stored")
        q_saved, k_saved = m.sem("q_saved"), m.sem("k_saved")
        stacked = [m.sems(f"stacked{h}_") for h in range(2)]
        row_loaded = [m.sems(f"row_loaded{h}_") for h in range(2)]
        xT_done, xhi_ready, xlo_ready = m.sem("xT_done"), m.sem("xhi_ready"), m.sem("xlo_ready")
        chi_ready, clo_ready = m.sem("chi_ready"), m.sem("clo_ready")
        k_done, q_done, v_done = m.sem("k_done"), m.sem("q_done"), m.sem("v_done")
        k_kept, q_kept, v_kept = m.sem("k_kept"), m.sem("q_kept"), m.sem("v_kept")
        v_padded = m.sem("v_padded")
        klo_ready, qlo_ready = m.sem("klo_ready"), m.sem("qlo_ready")
        max_done, max_kept = m.sem("max_done"), m.sem("max_kept")
        maxT_done, maxT_kept = m.sem("maxT_done"), m.sem("maxT_kept")
        score_done, prob_ready, pv_done = m.sem("score_done"), m.sem("prob_ready"), m.sem("pv_done")
        inv_ready, o_ready, ohi_ready, olo_ready = (m.sem("inv_ready"), m.sem("o_ready"),
                                                    m.sem("ohi_ready"), m.sem("olo_ready"))
        res_ready, y_done, r_ready = m.sem("res_ready"), m.sem("y_done"), m.sem("r_ready")
        stat_ready, mean_ready, eps_ready = m.sem("stat_ready"), m.sem("mean_ready"), m.sem("eps_ready")
        rstd_ready, out_ready = m.sem("rstd_ready"), m.sem("out_ready")

        x_rows = x_in.rearrange("(b q p) d -> b p q d", q=QT, p=P)
        o_rows = x_out.rearrange("(b q p) d -> b p q d", q=QT, p=P)
        c_rows = ctx_t.rearrange("b (k p) s -> b p k s", p=P)

        def head(s):
            return HALF * (s // HALF) + 2 * (s % 4) + (s % HALF) // 4

        run = lambda eng, body: batches(eng, body, -2, B, 3, 4)
        block = m.block()

        @block.sync
        def _(sp):
            sp.dma_start(w_all[:], weights).then_inc(consts_loaded, 16)
            sp.dma_start(ident[:], consts["ident"]).then_inc(consts_loaded, 16)
            sp.dma_start(identb[:], consts["identb"]).then_inc(consts_loaded, 16)
            sp.dma_start(mask[:], consts["mask"]).then_inc(consts_loaded, 16)
            sp.dma_start(ones[:], consts["ones"]).then_inc(consts_loaded, 16)
            sp.dma_start(bvo[:], biases.partition_broadcast(P)).then_inc(consts_loaded, 16)
            if has_qkv_bias:
                sp.dma_start(bqk[:], bias_cols).then_inc(consts_loaded, 16)

            def load(st, d):
                p = st.parity(d)
                sp.dma_start(x_tok[p][:], x_rows[st.at(d)]).then_inc(x_loaded[p], 16)
                sp.dma_start(c_t[p][:], c_rows[st.at(d)]).then_inc(c_loaded[p], 16)

            def row_of(p, half):
                row = q_stack[p][STK:STK + 1, half * HALF:(half + 1) * HALF, :].bitcast(F32)
                return row.rearrange("o h (q t) -> o (h q) t", q=QT)

            def load_stack(st, half):
                p = st.parity(2)
                h0 = half * HALF
                rows = qk_dram[p].rearrange("w l (h e) s -> w l e h s", e=HD)
                for copy in range(2):
                    for l in range(2):
                        at = (2 * copy + l) * HD
                        sp.dma_start(k_stack[p][at:at + HD, h0:h0 + HALF, :].bitcast(F32),
                                     rows[0, l, :, h0:h0 + HALF, :]).then_inc(stacked[half][p], 16)
                        sp.dma_start(q_stack[p][at:at + HD, h0:h0 + HALF, :].bitcast(F32),
                                     rows[1, copy, :, h0:h0 + HALF, :]).then_inc(stacked[half][p], 16)
                sp.dma_start(row_of(p, half), zero_row[:]).then_inc(stacked[half][p], 16)

            sp.wait_ge(zeroed, 7)
            load(Step(0, -2), 2)

            def body(st):
                p2, p1 = st.parity(2), st.parity(1)
                if st.has(3):
                    if st.has(1):
                        sp.wait_ge(xT_done, st.done(1))
                        sp.wait_ge(chi_ready, st.done(1))
                        sp.wait_ge(clo_ready, st.done(1))
                    load(st, 3)
                if st.has(2):
                    sp.wait_ge(klo_ready, st.done(2))
                    sp.dma_start(qk_dram[p2][0].rearrange("l (k p) s -> p l k s", p=P),
                                 k_split[:].bitcast(F32)).then_inc(k_saved, 16)
                    sp.wait_ge(qlo_ready, st.done(2))
                    sp.dma_start(qk_dram[p2][1].rearrange("l (k p) s -> p l k s", p=P),
                                 q_split[:].bitcast(F32)).then_inc(q_saved, 16)
                if st.has(-1):
                    sp.dma_start(x_res[p1][:], x_rows[st.at(-1)]).then_inc(res_loaded[p1], 16)
                if st.has(2):
                    sp.wait_ge(k_saved, st.done(2) * 16)
                    sp.wait_ge(q_saved, st.done(2) * 16)
                    if st.has(0):
                        sp.wait_ge(score_done, st.at(0) * H + HALF)
                    load_stack(st, 0)
                if st.has(-1):
                    sp.wait_ge(out_ready, st.done(-1))
                    sp.dma_start(o_rows[st.at(-1)], y_out[p1][:]).then_inc(stored[p1], 16)
                for half in range(2):
                    if half == 1 and st.has(2):
                        if st.has(0):
                            sp.wait_ge(score_done, st.at(0) * H + H)
                        load_stack(st, 1)
                    if st.has(1):
                        sp.wait_ge(maxT_kept, st.at(1) * 2 + half + 1)
                        sp.wait_ge(stacked[half][p1], (st.nth(1) + 1) * 9 * 16)
                        sp.dma_start(row_of(p1, half),
                                     max_row[:, half, :].bitcast(F32)).then_inc(row_loaded[half][p1], 16)

            run(sp, body)
            for p in range(2):
                sp.wait_ge(stored[p], B // 2 * 16)

        @block.tensor
        def _(pe):
            wt = lambda i, k: (w_hi[:, i, k, :], w_lo[:, i, k, :])
            pe.wait_ge(consts_loaded, (7 if has_qkv_bias else 6) * 16)
            pe.wait_ge(w_hi_ready, 1)
            pe.wait_ge(w_lo_ready, 1)
            pe.wait_ge(zeroed, 7)

            def transpose_x(st):
                p = st.parity(2)
                pe.wait_ge(x_loaded[p], (st.nth(2) + 1) * 16)
                if st.has(0):
                    pe.wait_ge(maxT_kept, 2 * st.done(0))
                elif st.has(1):
                    pe.wait_ge(q_kept, 2 * st.done(1))
                for k in range(KT):
                    for q in range(QT):
                        last = pe.transpose(misc[0][:, k * S + q * P:k * S + (q + 1) * P],
                                            x_tok[p][:, q, k * P:(k + 1) * P], ident[:])
                last.then_inc(xT_done, 1)

            def project(bank, w, hi, lo, done):
                for f in range(KT):
                    for k in range(KT):
                        cols = slice(f * P, (f + 1) * P)
                        last = product3(pe, bank[:, f * S:(f + 1) * S],
                                        (w_hi[:, w, k, cols], w_lo[:, w, k, cols]),
                                        (hi[:, k, :], lo[:, k, :]), k == 0, k == KT - 1)
                last.then_inc(done, 1)

            def rows_product(bank, w, hi, lo, done):
                for q in range(QT):
                    for k in range(KT):
                        cols = slice(q * P, (q + 1) * P)
                        last = product3(pe, bank[:, q * D:(q + 1) * D],
                                        (hi[:, k, cols], lo[:, k, cols]), wt(w, k), k == 0, k == KT - 1)
                last.then_inc(done, 1)

            def project_k(st):
                pe.wait_ge(chi_ready, st.done(2))
                pe.wait_ge(clo_ready, st.done(2))
                if st.has(-2):
                    pe.wait_ge(r_ready, st.done(-2))
                elif st.has(1):
                    pe.wait_ge(v_kept, st.done(1))
                project(misc[1], 1, c_hi, c_lo, k_done)

            def project_q(st):
                pe.wait_ge(xhi_ready, st.done(2))
                pe.wait_ge(xlo_ready, st.done(2))
                project(misc[0], 0, x_hi, x_lo, q_done)

            def project_v(st):
                pe.wait_ge(k_kept, 2 * st.done(2))
                rows_product(misc[1], 2, c_hi, c_lo, v_done)

            def output(st):
                pe.wait_ge(v_kept, st.done(2))
                pe.wait_ge(ohi_ready, 2 * st.done(-1))
                pe.wait_ge(olo_ready, 2 * st.done(-1))
                rows_product(misc[1], 3, o_hi, o_lo, y_done)

            def max_scores(st, s):
                p, h = st.parity(1), head(s)
                if s % HALF == 0:
                    pe.wait_ge(stacked[s // HALF][p], (st.nth(1) + 1) * 9 * 16)
                n = st.at(1) * H + s
                bank = max_ps[s % 2]
                if s >= 2 or st.has(0):
                    pe.wait_ge(max_kept, n - 1)
                for q in range(QT):
                    last = pe.matmul(bank[:, q * S:(q + 1) * S], q_stack[p][:, h, q * P:(q + 1) * P],
                                     k_stack[p][:, h, :], start=True, stop=True,
                                     skip_group_check=causal)
                    if causal:
                        last = pe.matmul(bank[:, q * S + q * P:q * S + (q + 1) * P], identb[:],
                                         mask[:, 1, :], start=False, stop=True, skip_group_check=True)
                last.then_inc(max_done, 1)

            def transpose_max(st, half):
                p = st.parity(1)
                pe.wait_ge(max_kept, st.at(1) * H + (half + 1) * HALF)
                if half == 0:
                    pe.wait_ge(q_kept, 2 * st.done(2))
                else:
                    pe.wait_ge(maxT_kept, st.at(1) * 2 + 1)
                pe.transpose(misc[0][0:HALF * QT, 0:P],
                             neg_max[p][:, half * HALF:(half + 1) * HALF, :].rearrange("p h q -> p (h q)"),
                             ident[:]).then_inc(maxT_done, 1)

            def scores(st, s):
                p, h = st.parity(0), head(s)
                if s % HALF == 0:
                    pe.wait_ge(row_loaded[s // HALF][p], (st.nth(0) + 1) * 16)
                n = st.at(0) * H + s
                bank = score_ps[s % 2]
                if s >= 2 or st.has(-1):
                    pe.wait_ge(prob_ready, n - 1)
                for i, k in enumerate((1, 0)):
                    last = pe.matmul(bank[:, i * S:(i + 1) * S], k_stack[p][:, h, k * P:(k + 1) * P],
                                     q_stack[p][:, h, :], start=True, stop=True,
                                     skip_group_check=causal)
                    if causal:
                        last = pe.matmul(bank[:, i * S + k * P:i * S + (k + 1) * P], identb[:],
                                         mask[:, 0, :], start=False, stop=True, skip_group_check=True)
                last.then_inc(score_done, 1)

            def weighted(st, g, part):
                p, tile, par = st.parity(0), g // 2, g % 2
                n = st.at(0) * 4 + g
                if part == 0:
                    pe.wait_ge(prob_ready, 4 * n + 4)
                    if par == 0:
                        if tile == 0 and g == 0:
                            pe.wait_ge(v_padded, 2 * st.done(0))
                        pe.wait_ge(o_ready, st.at(0) * 2 + tile - 1) if st.has(-1) else None
                k = part % 2
                first_q = P if causal and k == 1 else 0
                cols = slice((1 - k) * S + first_q, (2 - k) * S)
                for quad in range(4):
                    rows = slice(32 * quad, 32 * quad + 32)
                    pair = tile * 4 + quad
                    if part < 2:
                        lhs, out0 = v_pad[p][:, k, pair, par, :, :].rearrange("p a e -> p (a e)"), 0
                    else:
                        lhs, out0 = ones[:, par, :], S
                    last = pe.matmul(out_ps[tile][rows, out0 + first_q:out0 + S], lhs,
                                     probs[g % 2][:, quad, cols], start=(par == 0 and part == 0),
                                     stop=(par == 1 and part == 3), skip_group_check=True)
                if part == 3:
                    last.then_inc(pv_done, 1)

            def body(st):
                if st.has(2):
                    transpose_x(st)
                    project_k(st)
                for s in range(H):
                    if st.has(0):
                        scores(st, s)
                    if st.has(1):
                        max_scores(st, s)
                    if st.has(0) and s >= 4:
                        weighted(st, s // 4 - 1, s % 4)
                    if s == 1 and st.has(2):
                        project_q(st)
                    if s == 3 and st.has(2):
                        project_v(st)
                    if s == 6 and st.has(-1):
                        output(st)
                    if s == 10 and st.has(1):
                        transpose_max(st, 0)
                if st.has(0):
                    for part in range(4):
                        weighted(st, 3, part)
                if st.has(1):
                    transpose_max(st, 1)

            run(pe, body)

        @block.scalar
        def _(act):
            act.wait_ge(consts_loaded, (7 if has_qkv_bias else 6) * 16)

            def keep(full, split, bank, done, kept, saved, st, col):
                act.wait_ge(done, st.done(2))
                if st.has(1):
                    act.wait_ge(saved, st.done(1) * 16)
                for dst, sem in ((full, kept), (split[:, 0], kept)):
                    if has_qkv_bias:
                        for f in range(KT):
                            last = nc.scalar.activation(dst[:, f, :], bank[:, f * S:(f + 1) * S],
                                                        ACT.Identity, bias=bqk[:, col + f:col + f + 1])
                    else:
                        last = nc.scalar.activation(dst.rearrange("p k s -> p (k s)") if dst is not full
                                                    else full[:, :, :].rearrange("p k s -> p (k s)"),
                                                    bank[:], ACT.Identity)
                    last.then_inc(sem, 1)

            def body(st):
                if st.has(2):
                    act.wait_ge(xT_done, st.done(2))
                    if st.has(1):
                        act.wait_ge(q_done, st.done(1))
                    nc.scalar.activation(x_hi[:].rearrange("p k s -> p (k s)"), misc[0][:],
                                         ACT.Identity).then_inc(xhi_ready, 1)
                for s in range(H):
                    if st.has(0):
                        n = st.at(0) * H + s
                        act.wait_ge(score_done, n + 1)
                        if s % 4 == 0 and (s >= 8 or st.has(-1)):
                            act.wait_ge(pv_done, st.at(0) * 4 + s // 4 - 1)
                        lo = P if causal else 0
                        nc.scalar.activation(probs[(s // 4) % 2][:, s % 4, lo:], score_ps[s % 2][:, lo:],
                                             ACT.Exp, scale=HD ** -0.5).then_inc(prob_ready, 1)
                    if s == 0 and st.has(2):
                        keep(k_full, k_split, misc[1], k_done, k_kept, k_saved, st, 2)
                    if s == 2 and st.has(2):
                        keep(q_full, q_split, misc[0], q_done, q_kept, q_saved, st, 0)
                    if s == 11 and st.has(1):
                        keep_max(st, 0)
                if st.has(1):
                    keep_max(st, 1)

            def keep_max(st, half):
                act.wait_ge(maxT_done, st.at(1) * 2 + half + 1)
                if st.has(0):
                    act.wait_ge(row_loaded[half][st.parity(0)], (st.nth(0) + 1) * 16)
                nc.scalar.activation(max_row[:, half, :], misc[0][0:HALF * QT, 0:P],
                                     ACT.Identity).then_inc(maxT_kept, 1)

            run(act, body)

        @block.vector
        def _(dve):
            dve.wait_ge(consts_loaded, (7 if has_qkv_bias else 6) * 16)
            dve.tensor_copy(w_hi[:], w_all[:]).then_inc(w_hi_ready, 1)
            for t in range(2):
                dve.memset(v_pad[t][:], 0.0).then_inc(v_zeroed, 1)
            dve.wait_ge(v_zeroed, 2)

            def take_max(st, s):
                n, p, h = st.at(1) * H + s, st.parity(1), head(s)
                dve.wait_ge(max_done, n + 1)
                bank = max_ps[s % 2]
                if s == 0 and st.has(-1):
                    dve.wait_ge(maxT_done, st.done(-1) * 2)
                if causal:
                    dve.tensor_reduce(neg_max[p][:, h, 0:1], bank[:, 0:P], AX.X, ALU.max, negate=True)
                    last = dve.tensor_reduce(neg_max[p][:, h, 1:2], bank[:, S:2 * S], AX.X, ALU.max,
                                             negate=True)
                else:
                    last = dve.tensor_reduce(neg_max[p][:, h, :], bank[:].rearrange("p (q k) -> p q k", q=QT),
                                             AX.X, ALU.max, negate=True)
                last.then_inc(max_kept, 1)

            def keep_v(st):
                dve.wait_ge(v_done, st.done(2))
                if st.has(1):
                    dve.wait_ge(v_padded, 2 * st.done(1))
                dve.tensor_copy(v_full[:].rearrange("p q d -> p (q d)"), misc[1][:]).then_inc(v_kept, 1)

            def normalize(st, d, tile):
                n = st.at(d) * 2 + tile
                dve.wait_ge(pv_done, st.at(d) * 4 + 2 * tile + 2)
                dve.reciprocal(inv_sum[:, tile, :], out_ps[tile][:, S:2 * S]).then_inc(inv_ready, 1)
                dve.wait_ge(inv_ready, n + 1)
                if st.has(d - 1):
                    dve.wait_ge(olo_ready, n - 1)
                    dve.wait_ge(y_done, st.done(d - 1))
                dve.tensor_tensor(o_full[:, tile, :], out_ps[tile][:, 0:S], inv_sum[:, tile, :],
                                  ALU.mult).then_inc(o_ready, 1)
                dve.wait_ge(o_ready, n + 1)
                dve.tensor_copy(o_hi[:, tile, :], o_full[:, tile, :]).then_inc(ohi_ready, 1)

            def norm_rows(st):
                n, p = st.done(-1), st.parity(-1)
                dve.wait_ge(y_done, n)
                dve.wait_ge(res_ready, n)
                dve.tensor_tensor(r[:].rearrange("p q d -> p (q d)"), misc[1][:],
                                  x_res[p][:].rearrange("p q d -> p (q d)"), ALU.add).then_inc(r_ready, 1)
                dve.wait_ge(r_ready, n)
                for q in range(QT):
                    dve.bn_stats(stats[:, q, :], r[:, q, :]).then_inc(stat_ready, 1)
                dve.wait_ge(stat_ready, 2 * n)
                dve.memset(gate[:], 0.0)
                for q in range(QT):
                    dve.bn_aggr(mv[:, q, :], stats[:, q, :]).then_inc(mean_ready, 1)
                dve.wait_ge(mean_ready, 2 * n)
                dve.tensor_scalar(var_eps[:], mv[:, :, 1], EPS, None, ALU.add).then_inc(eps_ready, 1)

            def finish_rows(st):
                n, p = st.done(-1), st.parity(-1)
                dve.wait_ge(rstd_ready, n)
                if st.has(-3):
                    dve.wait_ge(stored[p], st.nth(-1) * 16)
                for q in range(QT):
                    last = dve.tensor_scalar(y_out[p][:, q, :], r[:, q, :], mv[:, q, 0:1], rstd[:, q:q + 1],
                                             ALU.subtract, ALU.mult)
                last.then_inc(out_ready, 1)

            def body(st):
                if st.has(2):
                    p = st.parity(2)
                    dve.wait_ge(c_loaded[p], (st.nth(2) + 1) * 16)
                    if st.has(1):
                        dve.wait_ge(v_done, st.done(1))
                    dve.tensor_copy(c_hi[:], c_t[p][:]).then_inc(chi_ready, 1)
                    dve.wait_ge(xhi_ready, st.done(2))
                    dve.tensor_tensor(x_lo[:].rearrange("p k s -> p (k s)"), misc[0][:],
                                      x_hi[:].bitcast(F32).rearrange("p k s -> p (k s)"),
                                      ALU.subtract).then_inc(xlo_ready, 1)
                for s in range(H):
                    if st.has(1):
                        take_max(st, s)
                    if s == 2 and st.has(-1):
                        normalize(st, -1, 1)
                    if s == 4 and st.has(2):
                        keep_v(st)
                    if s == 7 and st.has(-1):
                        norm_rows(st)
                    if s == 9 and st.has(-1):
                        finish_rows(st)
                    if s == 13 and st.has(0):
                        normalize(st, 0, 0)

            run(dve, body)

        @block.gpsimd
        def _(pool):
            stacks = [stk for pair in zip(q_stack, k_stack) for stk in pair]
            for n, stk in enumerate(stacks):
                pool.memset(stk[STK:, :, :].bitcast(F32), 0.0).then_inc(zeroed, 1)
                pool.wait_ge(zeroed, n + 1)
            for t in range(2):
                pool.memset(k_stack[t][STK:STK + 1, :, :].bitcast(F32), 1.0).then_inc(zeroed, 1)
                pool.wait_ge(zeroed, t + 5)
            pool.memset(zero_row[:], 0.0).then_inc(zeroed, 1)
            pool.wait_ge(zeroed, 7)
            pool.memset(neg_half[:], -0.5).then_inc(zeroed, 1)
            pool.wait_ge(zeroed, 8)
            pool.wait_ge(consts_loaded, (7 if has_qkv_bias else 6) * 16)
            pool.wait_ge(w_hi_ready, 1)
            pool.tensor_tensor(w_lo[:], w_all[:], w_hi[:].bitcast(F32), ALU.subtract).then_inc(w_lo_ready, 1)

            def pad_v(st):
                p = st.parity(1)
                pool.wait_ge(v_kept, st.done(1))
                if st.has(-1):
                    pool.wait_ge(pv_done, 4 * st.done(-1))
                for par in range(2):
                    for k in range(QT):
                        src, bias = (z.rearrange("p (h a e) -> p h a e", a=2, e=HD)[:, :, par, :]
                                     for z in (v_full[:, k, :], bvo[:, 0, :]))
                        last = pool.tensor_tensor(v_pad[p][:, k, :, par, par, :], src, bias, ALU.add)
                    last.then_inc(v_padded, 1)

            def body(st):
                if st.has(1):
                    pad_v(st)
                if st.has(2):
                    p, n = st.parity(2), st.done(2)
                    pool.wait_ge(chi_ready, n)
                    pool.tensor_tensor(c_lo[:], c_t[p][:], c_hi[:].bitcast(F32), ALU.subtract).then_inc(clo_ready, 1)
                    pool.wait_ge(k_kept, 2 * n)
                    pool.tensor_tensor(k_split[:, 1], k_full[:], k_split[:, 0].bitcast(F32),
                                       ALU.subtract).then_inc(klo_ready, 1)
                    pool.wait_ge(q_kept, 2 * n)
                    pool.tensor_tensor(q_split[:, 1], q_full[:], q_split[:, 0].bitcast(F32),
                                       ALU.subtract).then_inc(qlo_ready, 1)
                if st.has(-1):
                    p, n = st.parity(-1), st.done(-1)
                    part_lo(st, -1, 1)
                    pool.wait_ge(res_loaded[p], (st.nth(-1) + 1) * 16)
                    for q in range(QT):
                        last = pool.tensor_tensor(x_res[p][:, q, :], x_res[p][:, q, :], bvo[:, 1, :], ALU.add)
                    last.then_inc(res_ready, 1)
                    pool.wait_ge(eps_ready, n)
                    pool.tensor_tensor(rstd[:], var_eps[:], neg_half[:], ALU.pow).then_inc(rstd_ready, 1)
                if st.has(0):
                    part_lo(st, 0, 0)

            def part_lo(st, d, tile):
                pool.wait_ge(ohi_ready, st.at(d) * 2 + tile + 1)
                pool.tensor_tensor(o_lo[:, tile, :], o_full[:, tile, :], o_hi[:, tile, :].bitcast(F32),
                                   ALU.subtract).then_inc(olo_ready, 1)

            run(pool, body)


def self_attention(nc, stage, x_in, x_out, weights, w_out, lambdas, coef_parts, lambda_init, consts):
    H = 32
    HALF, TILES, JQ, JK, GROUPS = 8, H // 8, 32, 8, 8
    STK = 4 * HD
    RESET = 8
    with ExitStack() as stack:
        m = Memory(nc, stack, stage)
        w_hi = m.sb("w_hi", [P, KT, 3 * D], F32R)
        w_lo = m.sb("w_lo", [P, KT, 3 * D], F32R)
        wo_hi = m.sb("wo_hi", [P, 6, D], F32R)
        wo_lo = m.sb("wo_lo", [P, 6, D], F32R)
        lam_in = m.sb("lam_in", [P, 4, P])
        lam_mul = m.sb("lam_mul", [P, 2, P])
        lam_sum = m.sb("lam_sum", [P, 2])
        lam_exp = m.sb("lam_exp", [P, 2])
        lam = m.sb("lam", [P, 2])
        parts = m.sb("parts", [P, 2])
        coef = m.sb("coef", [P, 1])
        ident = m.sb("ident", [P, P])
        identb = m.sb("identb", [P, P], BF16)
        mask = m.sb("mask", [P, 2, P], BF16)
        ones = m.sb("ones", [P, 2, 32])
        x_tok = [m.sb(f"x_tok{i}", [P, QT, D]) for i in range(2)]
        x_hi = m.sb("x_hi", [P, KT, S], F32R)
        x_lo = m.sb("x_lo", [P, KT, S], F32R)
        q_split = m.sb("q_split", [P, 2, 4, S], F32R)
        k_split = m.sb("k_split", [P, 2, S], F32R)
        v_tok = m.sb("v_tok", [P, QT, P])
        v_nat = m.sb("v_nat", [P, 2 * GROUPS, HD])
        v_pad = [m.sb(f"v_pad{i}", [P, 2 * GROUPS, 2, 2, HD]) for i in range(2)]
        q_raw = m.sb("q_raw", [P, JQ, P])
        k_raw = m.sb("k_raw", [STK, JK, S])
        q_stack = [m.sb(f"q_stack{i}", [P, H, S], F32R) for i in range(2)]
        zero_row = m.sb("zero_row", [HALF * QT, P])
        k_stack = [m.sb(f"k_stack{i}", [P, GROUPS, S], F32R) for i in range(2)]
        neg_max = [m.sb(f"neg_max{i}", [P, H, QT]) for i in range(2)]
        max_row = m.sb("max_row", [HALF * QT, TILES, P], F32R)
        probs = [m.sb(f"probs{i}", [P, 4, 2 * S]) for i in range(2)]
        wo_all, w_all = (t[:].rearrange("p a b -> p (a b)")[:, 0:6 * D] for t in probs)
        wo_all = wo_all.rearrange("p (k d) -> p k d", d=D)
        w_all = w_all.rearrange("p (k d) -> p k d", k=KT)
        inv_sum = m.sb("inv_sum", [P, 2, S])
        o_full = m.sb("o_full", [P, 2, S])
        o_hi = m.sb("o_hi", [P, TILES, S], F32R)
        o_lo = m.sb("o_lo", [P, TILES, S], F32R)
        y_hi = m.sb("y_hi", [P, QT, D], F32R)
        y_lo = m.sb("y_lo", [P, QT, D], F32R)
        x_res = [m.sb(f"x_res{i}", [P, QT, D]) for i in range(2)]
        r = m.sb("r", [P, QT, D])
        stats = m.sb("stats", [P, QT, 6])
        gate = m.sb("gate", [P, 1])
        mv = m.sb("mv", [P, QT, 2])
        neg_half = m.sb("neg_half", [P, QT])
        var_eps = m.sb("var_eps", [P, QT])
        rstd = m.sb("rstd", [P, QT])
        y_out = [m.sb(f"y_out{i}", [P, QT, D]) for i in range(2)]

        misc = [m.ps(f"misc{i}") for i in range(2)]
        max_ps = [m.ps(f"max_ps{i}") for i in range(2)]
        score_ps = [m.ps(f"score_ps{i}") for i in range(2)]
        out_ps = [m.ps(f"out_ps{i}") for i in range(2)]

        q_dram = [nc.dram_tensor(f"{stage}_q{i}", (2, 2 * D, S), F32, kind="Internal").ap() for i in range(2)]
        k_dram = [nc.dram_tensor(f"{stage}_k{i}", (2, P, S), F32, kind="Internal").ap() for i in range(2)]
        v_dram = [nc.dram_tensor(f"{stage}_v{i}", (S, P), F32, kind="Internal").ap() for i in range(2)]

        consts_loaded, coef_loaded = m.sem("consts_loaded"), m.sem("coef_loaded")
        w_hi_ready, w_lo_ready = m.sem("w_hi_ready"), m.sem("w_lo_ready")
        lam_step, lam_exp_ready, coef_ready = m.sem("lam_step"), m.sem("lam_exp_ready"), m.sem("coef_ready")
        zeroed, v_zeroed = m.sem("zeroed"), m.sem("v_zeroed")
        x_loaded, res_loaded, stored = m.sems("x_loaded"), m.sems("res_loaded"), m.sems("stored")
        q_saved, k_saved, v_saved, v_loaded = (m.sem("q_saved"), m.sem("k_saved"), m.sem("v_saved"),
                                               m.sem("v_loaded"))
        q_landed, k_landed = m.sems("q_landed"), m.sem("k_landed")
        row_zeroed = m.sems("row_zeroed", TILES)
        q_sorted, k_sorted = m.sem("q_sorted"), m.sem("k_sorted")
        row_loaded = [m.sems(f"row_loaded{h}_") for h in range(TILES)]
        xT_done, xhi_ready, xlo_ready = m.sem("xT_done"), m.sem("xhi_ready"), m.sem("xlo_ready")
        k_done, q_done, v_done = m.sem("k_done"), m.sem("q_done"), m.sem("v_done")
        qhi_ready, khi_ready = m.sem("qhi_ready"), m.sem("khi_ready")
        klo_ready, qlo_ready, v_kept, v_padded = (m.sem("klo_ready"), m.sem("qlo_ready"),
                                                  m.sem("v_kept"), m.sem("v_padded"))
        max_done, max_kept = m.sem("max_done"), m.sem("max_kept")
        maxT_done, maxT_kept = m.sem("maxT_done"), m.sem("maxT_kept")
        score_done, prob_ready, pv_done = m.sem("score_done"), m.sem("prob_ready"), m.sem("pv_done")
        inv_ready, o_ready, ohi_ready, olo_ready = (m.sem("inv_ready"), m.sem("o_ready"),
                                                    m.sem("ohi_ready"), m.sem("olo_ready"))
        y1_done, yhi_ready, ylo_ready, y_done = (m.sem("y1_done"), m.sem("yhi_ready"),
                                                 m.sem("ylo_ready"), m.sem("y_done"))
        r_ready, stat_ready, mean_ready, eps_ready = (m.sem("r_ready"), m.sem("stat_ready"),
                                                      m.sem("mean_ready"), m.sem("eps_ready"))
        rstd_ready, out_ready = m.sem("rstd_ready"), m.sem("out_ready")

        x_rows = x_in.rearrange("(b q p) d -> b p q d", q=QT, p=P)
        o_rows = x_out.rearrange("(b q p) d -> b p q d", q=QT, p=P)

        def head(s):
            return HALF * (s // HALF) + 2 * (s % 4) + (s % HALF) // 4

        def q_cols(p, h, q=None):
            return q_stack[p][:, h, :] if q is None else q_stack[p][:, h, q * P:(q + 1) * P]

        def k_cols(p, h, k=None):
            return k_stack[p][:, h // 4, :] if k is None else k_stack[p][:, h // 4, k * P:(k + 1) * P]

        run = lambda eng, body: batches(eng, body, -2, B, 3, 4)
        block = m.block()

        @block.sync
        def _(sp):
            sp.dma_start(lam_in[:], lambdas.partition_broadcast(P)).then_inc(coef_loaded, 16)
            sp.dma_start(parts[:], coef_parts).then_inc(coef_loaded, 16)
            sp.dma_start(w_all, weights).then_inc(consts_loaded, 16)
            sp.dma_start(wo_all, w_out).then_inc(consts_loaded, 16)
            sp.dma_start(ident[:], consts["ident"]).then_inc(consts_loaded, 16)
            sp.dma_start(identb[:], consts["identb"]).then_inc(consts_loaded, 16)
            sp.dma_start(mask[:], consts["mask"]).then_inc(consts_loaded, 16)
            sp.dma_start(ones[:], consts["ones"]).then_inc(consts_loaded, 16)

            def load(st, d):
                p = st.parity(d)
                sp.dma_start(x_tok[p][:], x_rows[st.at(d)]).then_inc(x_loaded[p], 16)

            def load_raw(st):
                p, n = st.parity(2), st.done(2)
                q_rows = q_dram[p].rearrange("l (j e) s -> l e j s", e=HD)
                k_rows = k_dram[p].rearrange("l (j e) s -> l e j s", e=HD)
                sp.wait_ge(k_saved, n * 16)
                if st.has(1):
                    sp.wait_ge(k_sorted, st.done(1))
                for i in range(4):
                    sp.dma_start(k_raw[i * HD:(i + 1) * HD], k_rows[i % 2]).then_inc(k_landed, 16)
                sp.wait_ge(q_saved, n * 16)
                for half in range(2):
                    if st.has(1):
                        sp.wait_ge(q_sorted, TILES * st.done(1) - 2 + 2 * half)
                    for i in range(4):
                        at = half * STK + i * HD
                        sp.dma_start(q_raw[at:at + HD],
                                     q_rows[i // 2, :, :, half * P:(half + 1) * P]).then_inc(q_landed[half], 16)

            sp.wait_ge(zeroed, RESET)
            load(Step(0, -2), 2)

            def body(st):
                p2, p1 = st.parity(2), st.parity(1)
                if st.has(3):
                    if st.has(1):
                        sp.wait_ge(xT_done, st.done(1))
                    load(st, 3)
                if st.has(-1):
                    sp.dma_start(x_res[p1][:], x_rows[st.at(-1)]).then_inc(res_loaded[p1], 16)
                if st.has(2):
                    n = st.done(2)
                    sp.wait_ge(qlo_ready, 2 * n)
                    sp.dma_start(q_dram[p2].rearrange("l (k p) s -> p l k s", p=P),
                                 q_split[:].bitcast(F32)).then_inc(q_saved, 16)
                    sp.wait_ge(klo_ready, n)
                    sp.dma_start(k_dram[p2].rearrange("l p s -> p l s"),
                                 k_split[:].bitcast(F32)).then_inc(k_saved, 16)
                    sp.wait_ge(v_kept, n)
                    sp.dma_start(v_dram[p2].rearrange("(q p) c -> p q c", p=P), v_tok[:]).then_inc(v_saved, 16)
                    load_raw(st)
                    if st.has(1):
                        sp.wait_ge(v_padded, 2 * st.done(1))
                    sp.wait_ge(v_saved, n * 16)
                    sp.dma_start(v_nat[:], v_dram[p2].rearrange("(n p) (j e) -> (n p j) e", p=16, e=HD)
                                 .rearrange("(n p) e -> p n e", p=P)).then_inc(v_loaded, 16)
                load_row(st, 0)
                if st.has(-1):
                    sp.wait_ge(out_ready, st.done(-1))
                    sp.dma_start(o_rows[st.at(-1)], y_out[p1][:]).then_inc(stored[p1], 16)
                for tile in range(1, TILES):
                    load_row(st, tile)

            def row_of(p, tile):
                row = q_stack[p][STK:STK + 1, tile * HALF:(tile + 1) * HALF, :].bitcast(F32)
                return row.rearrange("o h (q t) -> o (h q) t", q=QT)

            def load_row(st, tile):
                if st.has(2):
                    if st.has(0):
                        sp.wait_ge(score_done, st.at(0) * H + (tile + 1) * HALF)
                    sp.dma_start(row_of(st.parity(2), tile), zero_row[:]).then_inc(row_zeroed[tile], 16)
                if st.has(1):
                    sp.wait_ge(maxT_kept, st.at(1) * TILES + tile + 1)
                    sp.dma_start(row_of(st.parity(1), tile),
                                 max_row[:, tile, :].bitcast(F32)).then_inc(row_loaded[tile][st.parity(1)], 16)

            run(sp, body)
            for p in range(2):
                sp.wait_ge(stored[p], B // 2 * 16)

        @block.tensor
        def _(pe):
            pe.wait_ge(consts_loaded, 6 * 16)
            pe.wait_ge(w_hi_ready, 2)
            pe.wait_ge(w_lo_ready, 2)
            pe.wait_ge(zeroed, RESET)

            def transpose_x(st):
                p = st.parity(2)
                pe.wait_ge(x_loaded[p], (st.nth(2) + 1) * 16)
                if st.has(0):
                    pe.wait_ge(maxT_kept, TILES * st.done(0))
                elif st.has(1):
                    pe.wait_ge(v_kept, st.done(1))
                for k in range(KT):
                    for q in range(QT):
                        last = pe.transpose(misc[0][:, k * S + q * P:k * S + (q + 1) * P],
                                            x_tok[p][:, q, k * P:(k + 1) * P], ident[:])
                last.then_inc(xT_done, 1)

            def project_q(st, part):
                if part == 0:
                    pe.wait_ge(xhi_ready, st.done(2))
                    if st.has(0):
                        pe.wait_ge(maxT_kept, TILES * st.done(0))
                    elif st.has(1):
                        pe.wait_ge(klo_ready, st.done(1))
                pe.wait_ge(xlo_ready, st.done(2))
                features(misc[1 - part], 2 * part, 2, q_done)

            def features(bank, f0, n, done):
                for f in range(n):
                    for k in range(KT):
                        cols = slice((f0 + f) * P, (f0 + f + 1) * P)
                        last = product3(pe, bank[:, f * S:(f + 1) * S], (w_hi[:, k, cols], w_lo[:, k, cols]),
                                        (x_hi[:, k, :], x_lo[:, k, :]), k == 0, k == KT - 1)
                last.then_inc(done, 1)

            def rows_product(bank, a_hi, a_lo, tiles, rhs, done):
                for q in range(QT):
                    for k in range(tiles):
                        cols = slice(q * P, (q + 1) * P)
                        last = product3(pe, bank[:, q * D:(q + 1) * D], (a_hi[:, k, cols], a_lo[:, k, cols]),
                                        rhs(k), k == 0, k == tiles - 1)
                last.then_inc(done, 1)

            def project_k(st):
                pe.wait_ge(qlo_ready, 2 * st.done(2) - 1)
                features(misc[1], 4, 1, k_done)

            def project_v(st):
                pe.wait_ge(qlo_ready, 2 * st.done(2))
                rows_product(misc[0], x_hi, x_lo, KT,
                             lambda k: (w_hi[:, k, 2 * D:], w_lo[:, k, 2 * D:]), v_done)

            def output_1(st):
                pe.wait_ge(v_kept, st.done(2))
                pe.wait_ge(ohi_ready, TILES * st.done(-1))
                pe.wait_ge(olo_ready, TILES * st.done(-1))
                rows_product(misc[0], o_hi, o_lo, TILES, lambda k: (wo_hi[:, k, :], wo_lo[:, k, :]), y1_done)

            def output_2(st):
                if st.has(1):
                    pe.wait_ge(maxT_kept, TILES * st.at(1) + 1)
                pe.wait_ge(yhi_ready, st.done(-1))
                pe.wait_ge(ylo_ready, st.done(-1))
                rows_product(misc[1], y_hi, y_lo, QT,
                             lambda k: (wo_hi[:, TILES + k, :], wo_lo[:, TILES + k, :]), y_done)

            def max_scores(st, s):
                p, h = st.parity(1), head(s)
                if s % HALF == 0:
                    pe.wait_ge(q_sorted, st.at(1) * TILES + s // HALF + 1)
                    pe.wait_ge(row_zeroed[s // HALF], st.done(1) * 16)
                    if s == 0:
                        pe.wait_ge(k_sorted, st.done(1))
                n = st.at(1) * H + s
                bank = max_ps[s % 2]
                if s >= 2 or st.has(0):
                    pe.wait_ge(max_kept, n - 1)
                for q in range(QT):
                    pe.matmul(bank[:, q * S:(q + 1) * S], q_cols(p, h, q), k_cols(p, h), start=True, stop=True,
                              skip_group_check=True)
                    last = pe.matmul(bank[:, q * S + q * P:q * S + (q + 1) * P], identb[:],
                                     mask[:, 1, :], start=False, stop=True, skip_group_check=True)
                last.then_inc(max_done, 1)

            def transpose_max(st, tile):
                p = st.parity(1)
                pe.wait_ge(max_kept, st.at(1) * H + (tile + 1) * HALF)
                if tile == 0:
                    pe.wait_ge(klo_ready, st.done(2))
                elif tile == 1:
                    pe.wait_ge(ylo_ready, st.done(-1)) if st.has(-1) else pe.wait_ge(v_kept, st.done(2))
                elif tile == 2 and st.has(-1):
                    pe.wait_ge(r_ready, st.done(-1))
                else:
                    pe.wait_ge(maxT_kept, st.at(1) * TILES + tile - 1)
                pe.transpose(misc[1 - tile % 2][0:HALF * QT, 0:P],
                             neg_max[p][:, tile * HALF:(tile + 1) * HALF, :].rearrange("p h q -> p (h q)"),
                             ident[:]).then_inc(maxT_done, 1)

            def scores(st, s):
                p, h = st.parity(0), head(s)
                if s % HALF == 0:
                    pe.wait_ge(row_loaded[s // HALF][p], (st.nth(0) + 1) * 16)
                n = st.at(0) * H + s
                bank = score_ps[s % 2]
                if s >= 2 or st.has(-1):
                    pe.wait_ge(prob_ready, n - 1)
                for i, k in enumerate((1, 0)):
                    pe.matmul(bank[:, i * S:(i + 1) * S], k_cols(p, h, k), q_cols(p, h), start=True, stop=True,
                              skip_group_check=True)
                    last = pe.matmul(bank[:, i * S + k * P:i * S + (k + 1) * P], identb[:],
                                     mask[:, 0, :], start=False, stop=True, skip_group_check=True)
                last.then_inc(score_done, 1)

            def weighted(st, g, part):
                p, tile, par = st.parity(0), g // 2, g % 2
                n = st.at(0) * 8 + g
                bank = out_ps[tile % 2]
                if part == 0:
                    pe.wait_ge(prob_ready, 4 * n + 4)
                    if par == 0:
                        if g == 0:
                            pe.wait_ge(v_padded, 2 * st.done(0))
                        if tile >= 2 or st.has(-1):
                            pe.wait_ge(o_ready, st.at(0) * TILES + tile - 1)
                k = part % 2
                first_q = P if k == 1 else 0
                cols = slice((1 - k) * S + first_q, (2 - k) * S)
                for quad in range(4):
                    rows = slice(32 * quad, 32 * quad + 32)
                    if part < 2:
                        lhs = v_pad[p][:, 2 * (2 * tile + quad // 2) + k, par, :, :].rearrange("p a e -> p (a e)")
                        out0 = 0
                    else:
                        lhs, out0 = ones[:, par, :], S
                    last = pe.matmul(bank[rows, out0 + first_q:out0 + S], lhs,
                                     probs[g % 2][:, quad, cols], start=(par == 0 and part == 0),
                                     stop=(par == 1 and part == 3), skip_group_check=True)
                if part == 3:
                    last.then_inc(pv_done, 1)

            def body(st):
                if st.has(2):
                    transpose_x(st)
                for s in range(H):
                    if st.has(0):
                        scores(st, s)
                    if st.has(1):
                        max_scores(st, s)
                    if st.has(0) and s >= 4:
                        weighted(st, s // 4 - 1, s % 4)
                    if st.has(2):
                        if s in (1, 3):
                            project_q(st, s // 2)
                        if s == 5:
                            project_k(st)
                        if s == 7:
                            project_v(st)
                    if st.has(-1):
                        if s == 12:
                            output_1(st)
                        if s == 16:
                            output_2(st)
                    if st.has(1) and s in (10, 18, 26):
                        transpose_max(st, s // 8 - 1)
                if st.has(0):
                    for part in range(4):
                        weighted(st, 7, part)
                if st.has(1):
                    transpose_max(st, 3)

            run(pe, body)

        @block.scalar
        def _(act):
            act.wait_ge(lam_step, 2)
            nc.scalar.activation(lam_exp[:], lam_sum[:], ACT.Exp).then_inc(lam_exp_ready, 1)

            def keep_max(st, tile):
                act.wait_ge(maxT_done, st.at(1) * TILES + tile + 1)
                if st.has(0):
                    act.wait_ge(row_loaded[tile][st.parity(0)], (st.nth(0) + 1) * 16)
                nc.scalar.activation(max_row[:, tile, :], misc[1 - tile % 2][0:HALF * QT, 0:P],
                                     ACT.Identity).then_inc(maxT_kept, 1)

            def sort_q(st, d, tile):
                p, half = st.parity(d), tile // 2
                act.wait_ge(q_landed[half], (st.at(d) + 1) * 64)
                if st.has(d - 2):
                    act.wait_ge(score_done, st.at(d - 2) * H + (tile + 1) * HALF)
                lo, heads = (tile % 2) * 64, slice(tile * HALF, (tile + 1) * HALF)
                nc.scalar.activation(
                    q_stack[p][0:STK, heads, :].rearrange("e h (i j) -> e (h i) j", i=8),
                    q_raw[half * STK:(half + 1) * STK, :, lo:lo + 64].rearrange("e j s -> e s j"), ACT.Identity).then_inc(q_sorted, 1)

            def body(st):
                if st.has(2):
                    act.wait_ge(xT_done, st.done(2))
                    if st.has(1):
                        act.wait_ge(v_done, st.done(1))
                    nc.scalar.activation(x_hi[:].rearrange("p k s -> p (k s)"), misc[0][:],
                                         ACT.Identity).then_inc(xhi_ready, 1)
                for s in range(H):
                    if st.has(0):
                        n = st.at(0) * H + s
                        act.wait_ge(score_done, n + 1)
                        if s % 4 == 0 and (s >= 8 or st.has(-1)):
                            act.wait_ge(pv_done, st.at(0) * 8 + s // 4 - 1)
                        nc.scalar.activation(probs[(s // 4) % 2][:, s % 4, P:], score_ps[s % 2][:, P:],
                                             ACT.Exp, scale=HD ** -0.5).then_inc(prob_ready, 1)
                    if st.has(2) and s in (2, 4):
                        part = s // 2 - 1
                        act.wait_ge(q_done, 2 * st.done(2) - 1 + part)
                        if st.has(1):
                            act.wait_ge(q_saved, st.done(1) * 16)
                        nc.scalar.activation(q_split[:, 0, 2 * part:2 * part + 2, :].rearrange("p k s -> p (k s)"),
                                             misc[1 - part][:], ACT.Identity).then_inc(qhi_ready, 1)
                    if st.has(2) and s == 6:
                        act.wait_ge(k_done, st.done(2))
                        if st.has(1):
                            act.wait_ge(k_saved, st.done(1) * 16)
                        nc.scalar.activation(k_split[:, 0, :], misc[1][:, 0:S], ACT.Identity).then_inc(khi_ready, 1)
                    if st.has(-1) and s == 13:
                        act.wait_ge(y1_done, st.done(-1))
                        if st.has(-2):
                            act.wait_ge(y_done, st.done(-2))
                        nc.scalar.activation(y_hi[:].rearrange("p q d -> p (q d)"), misc[0][:],
                                             ACT.Identity).then_inc(yhi_ready, 1)
                    if st.has(1) and s in (11, 19, 27):
                        keep_max(st, s // 8 - 1)
                    if st.has(1) and s == 2:
                        sort_q(st, 1, 3)
                    if st.has(2) and s in (15, 20, 25):
                        sort_q(st, 2, s // 5 - 3)
                if st.has(1):
                    keep_max(st, 3)

            run(act, body)

        @block.vector
        def _(dve):
            dve.wait_ge(coef_loaded, 32)
            pairs = lam_in[:].rearrange("p (a b) c -> p a b c", b=2)
            dve.tensor_tensor(lam_mul[:], pairs[:, :, 0, :], pairs[:, :, 1, :], ALU.mult).then_inc(lam_step, 1)
            dve.wait_ge(lam_step, 1)
            dve.tensor_reduce(lam_sum[:], lam_mul[:], AX.X, ALU.add).then_inc(lam_step, 1)
            dve.wait_ge(consts_loaded, 6 * 16)
            dve.tensor_copy(w_hi[:], w_all).then_inc(w_hi_ready, 1)
            dve.wait_ge(lam_exp_ready, 1)
            dve.tensor_tensor(lam[:, 0:1], lam_exp[:, 0:1], lam_exp[:, 1:2], ALU.subtract).then_inc(lam_step, 1)
            dve.wait_ge(lam_step, 3)
            dve.tensor_scalar(lam[:, 1:2], lam[:, 0:1], lambda_init, None, ALU.add).then_inc(lam_step, 1)
            dve.wait_ge(lam_step, 4)
            dve.scalar_tensor_tensor(coef[:], parts[:, 1:2], lam[:, 1:2], parts[:, 0:1],
                                     ALU.mult, ALU.add).then_inc(lam_step, 1)
            dve.wait_ge(lam_step, 5)
            dve.tensor_scalar(wo_all[:, 0:TILES, :], wo_all[:, 0:TILES, :], coef[:, 0:1], None,
                              ALU.mult).then_inc(coef_ready, 1)
            dve.wait_ge(coef_ready, 1)
            dve.tensor_copy(wo_hi[:], wo_all).then_inc(w_hi_ready, 1)
            for t in range(2):
                dve.memset(v_pad[t][:], 0.0).then_inc(v_zeroed, 1)

            def take_max(st, s):
                n, p, h = st.at(1) * H + s, st.parity(1), head(s)
                dve.wait_ge(max_done, n + 1)
                bank = max_ps[s % 2]
                if s == 0 and st.has(-1):
                    dve.wait_ge(maxT_done, st.done(-1) * TILES)
                dve.tensor_reduce(neg_max[p][:, h, 0:1], bank[:, 0:P], AX.X, ALU.max, negate=True)
                dve.tensor_reduce(neg_max[p][:, h, 1:2], bank[:, S:2 * S], AX.X, ALU.max,
                                  negate=True).then_inc(max_kept, 1)

            def normalize(st, d, tile):
                n, b = st.at(d) * TILES + tile, tile % 2
                dve.wait_ge(pv_done, st.at(d) * 8 + 2 * tile + 2)
                dve.reciprocal(inv_sum[:, b, :], out_ps[b][:, S:2 * S]).then_inc(inv_ready, 1)
                dve.wait_ge(inv_ready, n + 1)
                if st.has(d - 1):
                    dve.wait_ge(y1_done, st.done(d - 1))
                if tile >= 2 or st.has(d - 1):
                    dve.wait_ge(olo_ready, n - 1)
                dve.tensor_tensor(o_full[:, b, :], out_ps[b][:, 0:S], inv_sum[:, b, :],
                                  ALU.mult).then_inc(o_ready, 1)
                dve.wait_ge(o_ready, n + 1)
                dve.tensor_copy(o_hi[:, tile, :], o_full[:, b, :]).then_inc(ohi_ready, 1)

            def keep_q_lo(st, part):
                dve.wait_ge(qhi_ready, 2 * st.done(2) - 1 + part)
                at = slice(2 * part, 2 * part + 2)
                dve.tensor_tensor(q_split[:, 1, at, :].rearrange("p k s -> p (k s)"), misc[1 - part][:],
                                  q_split[:, 0, at, :].bitcast(F32).rearrange("p k s -> p (k s)"),
                                  ALU.subtract).then_inc(qlo_ready, 1)

            def sort_k(st):
                p = st.parity(2)
                dve.wait_ge(k_landed, st.done(2) * 64)
                if st.has(0):
                    dve.wait_ge(score_done, st.at(0) * H + H)
                dve.tensor_copy(k_stack[p][0:STK].rearrange("e g (s j) -> e (g s) j", j=JK),
                                k_raw[:].rearrange("e j s -> e s j")).then_inc(k_sorted, 1)

            def norm_rows(st):
                n, p = st.done(-1), st.parity(-1)
                dve.wait_ge(y_done, n)
                dve.wait_ge(res_loaded[p], (st.nth(-1) + 1) * 16)
                dve.tensor_tensor(r[:].rearrange("p q d -> p (q d)"), misc[1][:],
                                  x_res[p][:].rearrange("p q d -> p (q d)"), ALU.add).then_inc(r_ready, 1)
                dve.wait_ge(r_ready, n)
                for q in range(QT):
                    dve.bn_stats(stats[:, q, :], r[:, q, :]).then_inc(stat_ready, 1)
                dve.wait_ge(stat_ready, 2 * n)
                dve.memset(gate[:], 0.0)
                for q in range(QT):
                    dve.bn_aggr(mv[:, q, :], stats[:, q, :]).then_inc(mean_ready, 1)
                dve.wait_ge(mean_ready, 2 * n)
                dve.tensor_scalar(var_eps[:], mv[:, :, 1], EPS, None, ALU.add).then_inc(eps_ready, 1)

            def finish_rows(st):
                n, p = st.done(-1), st.parity(-1)
                dve.wait_ge(rstd_ready, n)
                if st.has(-3):
                    dve.wait_ge(stored[p], st.nth(-1) * 16)
                for q in range(QT):
                    last = dve.tensor_scalar(y_out[p][:, q, :], r[:, q, :], mv[:, q, 0:1], rstd[:, q:q + 1],
                                             ALU.subtract, ALU.mult)
                last.then_inc(out_ready, 1)

            def body(st):
                if st.has(2):
                    dve.wait_ge(xhi_ready, st.done(2))
                    dve.tensor_tensor(x_lo[:].rearrange("p k s -> p (k s)"), misc[0][:],
                                      x_hi[:].bitcast(F32).rearrange("p k s -> p (k s)"),
                                      ALU.subtract).then_inc(xlo_ready, 1)
                for s in range(H):
                    if st.has(1):
                        take_max(st, s)
                    if st.has(2):
                        if s in (2, 4):
                            keep_q_lo(st, s // 2 - 1)
                        if s == 6:
                            dve.wait_ge(khi_ready, st.done(2))
                            dve.tensor_tensor(k_split[:, 1, :], misc[1][:, 0:S], k_split[:, 0, :].bitcast(F32),
                                              ALU.subtract).then_inc(klo_ready, 1)
                        if s == 8:
                            dve.wait_ge(v_done, st.done(2))
                            if st.has(1):
                                dve.wait_ge(v_saved, st.done(1) * 16)
                            dve.tensor_copy(v_tok[:], misc[0][:].rearrange("p (q c) -> p q c", q=QT)[:, :, P:])\
                               .then_inc(v_kept, 1)
                    if st.has(-1):
                        if s == 1:
                            normalize(st, -1, TILES - 1)
                        if s == 14:
                            dve.wait_ge(yhi_ready, st.done(-1))
                            dve.tensor_tensor(y_lo[:].rearrange("p q d -> p (q d)"), misc[0][:],
                                              y_hi[:].bitcast(F32).rearrange("p q d -> p (q d)"),
                                              ALU.subtract).then_inc(ylo_ready, 1)
                        if s == 17:
                            norm_rows(st)
                        if s == 20:
                            finish_rows(st)
                    if st.has(0) and s in (13, 21, 29):
                        normalize(st, 0, s // 8 - 1)

                if st.has(2):
                    sort_k(st)
            run(dve, body)

        @block.gpsimd
        def _(pool):
            fills = [(stk[STK:, :, :].bitcast(F32), 0.0) for stk in q_stack + k_stack]
            fills += [(stk[STK:STK + 1, :, :].bitcast(F32), 1.0) for stk in k_stack]
            fills += [(zero_row[:], 0.0), (neg_half[:], -0.5)]
            for n, (what, value) in enumerate(fills):
                pool.memset(what, value).then_inc(zeroed, 1)
                pool.wait_ge(zeroed, n + 1)
            pool.wait_ge(w_hi_ready, 1)
            pool.tensor_tensor(w_lo[:], w_all, w_hi[:].bitcast(F32), ALU.subtract).then_inc(w_lo_ready, 1)
            pool.wait_ge(w_hi_ready, 2)
            pool.tensor_tensor(wo_lo[:], wo_all, wo_hi[:].bitcast(F32), ALU.subtract).then_inc(w_lo_ready, 1)
            pool.wait_ge(v_zeroed, 2)

            def part_lo(st, d, tile):
                pool.wait_ge(ohi_ready, st.at(d) * TILES + tile + 1)
                pool.tensor_tensor(o_lo[:, tile, :], o_full[:, tile % 2, :], o_hi[:, tile, :].bitcast(F32),
                                   ALU.subtract).then_inc(olo_ready, 1)

            def pad_v(st):
                p = st.parity(1)
                pool.wait_ge(v_loaded, 16 * st.done(1))
                if st.has(-1):
                    pool.wait_ge(pv_done, 8 * st.done(-1))
                for par in range(2):
                    zeros = v_pad[p][:, :, par, 1 - par, :]
                    pool.tensor_tensor(v_pad[p][:, :, par, par, :], v_nat[:], zeros,
                                       ALU.add).then_inc(v_padded, 1)

            def body(st):
                if st.has(-1):
                    part_lo(st, -1, TILES - 1)
                if st.has(1):
                    pad_v(st)
                if st.has(0):
                    part_lo(st, 0, 0)
                if st.has(-1):
                    pool.wait_ge(eps_ready, st.done(-1))
                    pool.tensor_tensor(rstd[:], var_eps[:], neg_half[:], ALU.pow).then_inc(rstd_ready, 1)
                if st.has(0):
                    part_lo(st, 0, 1)
                    part_lo(st, 0, 2)

            run(pool, body)


NE, TOP, FF = 8, 2, 512
TILE = 512
TQ = TILE // P
SHARED_HALF = B * S // TILE // 2
ROUTED = B * S * TOP // TILE + NE - 1
ALL_TILES = ROUTED + 2 * SHARED_HALF
WROW = 2 * KT * FF + (FF // P) * D


def mixture_of_experts(nc, stage, x_in, x_out, x_tiles, prefilled, swdge, router, router_bias, experts, tables, consts):
    NT = B * QT
    WT = FF // P
    slot0 = SHARED_HALF * TILE
    y_tiles = nc.dram_tensor(f"{stage}_y_tiles", (ALL_TILES * TILE, D), F32, kind="Internal").ap()

    with ExitStack() as outer:
        keep = Memory(nc, outer, stage + "k")
        x_tok = keep.sb("x_tok", [P, NT, D])
        slot = [keep.sb(f"slot{k}", [P, NT], U32) for k in range(TOP)]
        weight = [keep.sb(f"weight{k}", [P, NT]) for k in range(TOP)]
        tile_expert = keep.sb("tile_expert", [P, ALL_TILES])
        ident = keep.sb("ident", [P, P])

        route(nc, stage + "r", x_in, x_tiles, x_tok, slot, weight, tile_expert, ident, router, router_bias,
              tables, consts, slot0)
        expert_tiles(nc, stage + "e", x_tiles, y_tiles, x_tok, slot, tile_expert, ident, experts, tables, prefilled,
                     swdge[0], swdge[1])
        combine(nc, stage + "c", x_in, x_out, y_tiles, slot, weight, swdge[2:4])


def route(nc, stage, x_in, x_tiles, x_tok, slot, weight, tile_expert, ident, router, router_bias, tables,
          consts, slot0):
    NT = B * QT
    with ExitStack() as stack:
        m = Memory(nc, stack, stage)
        w = m.sb("w", [P, KT, NE])
        bias = m.sb("bias", [P, NE])
        table = m.sb("table", [P, 4 * P])
        before, ones = table[:, 0:P], table[:, P:2 * P]
        falling = table[:, 2 * P:2 * P + NE]
        steps = table[:, 2 * P + NE:2 * P + 2 * NE]
        tile_no = table[:, 2 * P + 2 * NE:2 * P + 2 * NE + ROUTED]
        xT = [m.sb(f"xT{i}", [P, KT, S]) for i in range(2)]
        full = lambda name: m.sb(name, [P, NT, NE])
        logit, mag, low, e_mag, e_low, den, prob = (full(n) for n in ("logit", "mag", "low", "e_mag", "e_low",
                                                                       "den", "prob"))
        hit, key, rest, both, mine, place = (full(n) for n in ("hit", "key", "rest", "both", "mine", "place"))
        sel = [full(f"sel{k}") for k in range(TOP)]
        total = [full(f"total{i}") for i in range(2)]
        own = full("own")
        top = [m.sb(f"top{k}", [P, NT]) for k in range(TOP)]
        slot_f = m.sb("slot_f", [P, NT])
        pick, den2, rden = m.sb("pick", [P, NT]), m.sb("den2", [P, NT]), m.sb("rden", [P, NT])
        over = m.sb("over", [P, NE, NE])
        ends = [m.sb(f"ends{i}", [P, NE]) for i in range(2)]
        tiles, start = m.sb("tiles", [P, NE]), m.sb("start", [P, NE])
        past, count = m.sb("past", [P, ROUTED, NE]), m.sb("count", [P, ROUTED])
        xT_ps = [m.ps(f"xT_ps{i}") for i in range(2)]
        logit_ps, prefix_ps, total_ps = m.ps("logit_ps"), m.ps("prefix_ps"), m.ps("total_ps")

        loaded, copied = m.sem("loaded"), m.sem("copied")
        GROUP = 4
        x_loaded = m.sems("x_loaded", B // GROUP)
        xT_done, xT_kept, logit_done = m.sem("xT_done"), m.sem("xT_kept"), m.sem("logit_done")
        logit_ready, mag_ready, exp_ready = m.sem("logit_ready"), m.sem("mag_ready"), m.sem("exp_ready")
        low_ready = m.sem("low_ready")
        both_ready, prefix_done, step_done = m.sem("both_ready"), m.sem("prefix_done"), m.sem("step_done")
        block = m.block()

        @block.sync
        def _(sp):
            for dst, src in ((w[:], router), (bias[:], router_bias.partition_broadcast(P)), (table[:], tables),
                             (ident[:], consts["ident"])):
                sp.dma_start(dst, src).then_inc(loaded, 16)
            x_rows = x_in.rearrange("(g q p) d -> g p q d", q=GROUP * QT, p=P)
            for g in range(B // GROUP):
                sp.dma_start(x_tok[:, g * GROUP * QT:(g + 1) * GROUP * QT, :], x_rows[g]).then_inc(x_loaded[g], 16)
            half = B * S // 2
            sp.dma_start(x_tiles[0:half, :], x_in[0:half, :]).then_inc(copied, 16)
            sp.dma_start(x_tiles[half + ROUTED * TILE:, :], x_in[half:, :]).then_inc(copied, 16)
            sp.wait_ge(copied, 32)

        @block.tensor
        def _(pe):
            pe.wait_ge(loaded, 4 * 16)

            def logits(b):
                pe.wait_ge(xT_kept, b + 1)
                for q in range(QT):
                    c = b * QT + q
                    for k in range(KT):
                        last = pe.matmul(logit_ps[:, c * NE:(c + 1) * NE], xT[b % 2][:, k, q * P:(q + 1) * P],
                                         w[:, k, :], start=k == 0, stop=k == KT - 1)
                last.then_inc(logit_done, 1)

            for b in range(B):
                pe.wait_ge(x_loaded[b // GROUP], 16)
                if b >= 2:
                    pe.wait_ge(xT_kept, b - 1)
                for k in range(KT):
                    for q in range(QT):
                        last = pe.transpose(xT_ps[b % 2][:, k * S + q * P:k * S + (q + 1) * P],
                                            x_tok[:, b * QT + q, k * P:(k + 1) * P], ident[:])
                last.then_inc(xT_done, 1)
                if b:
                    logits(b - 1)
            logits(B - 1)
            pe.wait_ge(both_ready, 1)
            flat = both[:].rearrange("p c e -> p (c e)")
            pe.matmul(prefix_ps[:, 0:NT * NE], before, flat, start=True, stop=True)
            pe.matmul(total_ps[:, 0:NT * NE], ones, flat, start=True, stop=True).then_inc(prefix_done, 1)

        @block.scalar
        def _(act):
            for b in range(B):
                act.wait_ge(xT_done, b + 1)
                if b >= 2:
                    act.wait_ge(logit_done, b - 1)
                nc.scalar.activation(xT[b % 2][:].rearrange("p k s -> p (k s)"), xT_ps[b % 2][:],
                                     ACT.Identity).then_inc(xT_kept, 1)
            act.wait_ge(logit_ready, 1)
            nc.scalar.activation(mag[:], logit[:], ACT.Abs).then_inc(mag_ready, 1)
            act.wait_ge(mag_ready, 1)
            nc.scalar.activation(e_mag[:], mag[:], ACT.Exp, scale=-1.0).then_inc(exp_ready, 1)
            act.wait_ge(low_ready, 1)
            nc.scalar.activation(e_low[:], low[:], ACT.Exp).then_inc(exp_ready, 1)

        @block.vector
        def _(dve):
            steps_done = [0]

            def then(instruction):
                instruction.then_inc(step_done, 1)
                steps_done[0] += 1
                dve.wait_ge(step_done, steps_done[0])

            by_token = lambda t: t[:].unsqueeze(2).broadcast_to([P, NT, NE])
            by_expert = lambda ap: ap.unsqueeze(1).broadcast_to([P, NT, NE])
            dve.wait_ge(loaded, 4 * 16)
            dve.wait_ge(logit_done, B)
            dve.tensor_tensor(logit[:], logit_ps[:, 0:NT * NE].rearrange("p (c e) -> p c e", e=NE),
                              by_expert(bias[:]), ALU.add).then_inc(logit_ready, 1)
            dve.wait_ge(logit_ready, 1)
            dve.tensor_scalar(low[:], logit[:], 0.0, None, ALU.min).then_inc(low_ready, 1)
            dve.wait_ge(exp_ready, 2)
            then(dve.tensor_scalar(den[:], e_mag[:], 1.0, None, ALU.add))
            then(dve.reciprocal(mag[:], den[:]))
            then(dve.tensor_tensor(prob[:], e_low[:], mag[:], ALU.mult))

            for k in range(TOP):
                if k:
                    then(dve.scalar_tensor_tensor(rest[:], sel[0][:], -2.0, prob[:], ALU.mult, ALU.add))
                source = (prob, rest)[k]
                then(dve.tensor_reduce(top[k][:], source[:], AX.X, ALU.max))
                then(dve.tensor_tensor(hit[:], source[:], by_token(top[k]), ALU.is_equal))
                then(dve.tensor_tensor(key[:], hit[:], by_expert(falling), ALU.mult))
                then(dve.tensor_reduce(pick[:], key[:], AX.X, ALU.max))
                then(dve.tensor_tensor(sel[k][:], key[:], by_token(pick), ALU.is_equal))
            dve.tensor_tensor(both[:], sel[0][:], sel[1][:], ALU.add).then_inc(both_ready, 1)
            then(dve.tensor_tensor(den2[:], top[0][:], top[1][:], ALU.add))
            then(dve.reciprocal(rden[:], den2[:]))
            for k in range(TOP):
                then(dve.tensor_tensor(weight[k][:], top[k][:], rden[:], ALU.mult))

            dve.wait_ge(prefix_done, 1)
            then(dve.tensor_copy(own[:].rearrange("p c e -> p (c e)"), total_ps[:, 0:NT * NE]))
            src, shift = own, 1
            while shift < NT:
                dst = total[0] if src is not total[0] else total[1]
                dve.tensor_copy(dst[:, 0:shift, :], src[:, 0:shift, :]).then_inc(step_done, 1)
                steps_done[0] += 1
                then(dve.tensor_tensor(dst[:, shift:, :], src[:, shift:, :], src[:, 0:NT - shift, :], ALU.add))
                src, shift = dst, 2 * shift
            chosen = src[:, NT - 1, :]
            then(dve.tensor_tensor(over[:], chosen.unsqueeze(2).broadcast_to([P, NE, NE]),
                                   steps.unsqueeze(1).broadcast_to([P, NE, NE]), ALU.is_gt))
            then(dve.tensor_reduce(tiles[:], over[:], AX.X, ALU.add))
            end, shift = tiles, 1
            while shift < NE:
                dst = ends[0] if end is not ends[0] else ends[1]
                dve.tensor_copy(dst[:, 0:shift], end[:, 0:shift]).then_inc(step_done, 1)
                steps_done[0] += 1
                then(dve.tensor_tensor(dst[:, shift:], end[:, shift:], end[:, 0:NE - shift], ALU.add))
                end, shift = dst, 2 * shift
            then(dve.tensor_tensor(start[:], end[:], tiles[:], ALU.subtract))
            then(dve.tensor_scalar(start[:], start[:], float(TILE), float(slot0), ALU.mult, ALU.add))
            then(dve.tensor_tensor(place[:], src[:], own[:], ALU.subtract))
            then(dve.tensor_tensor(place[:], place[:], by_expert(start[:]), ALU.add))
            then(dve.tensor_tensor(place[:], place[:], prefix_ps[:, 0:NT * NE].rearrange("p (c e) -> p c e", e=NE),
                                   ALU.add))
            for k in range(TOP):
                then(dve.tensor_tensor(mine[:], sel[k][:], place[:], ALU.mult))
                then(dve.tensor_reduce(slot_f[:], mine[:], AX.X, ALU.add))
                then(dve.tensor_copy(slot[k][:], slot_f[:]))
            then(dve.tensor_tensor(past[:], end[:].unsqueeze(1).broadcast_to([P, ROUTED, NE]),
                                   tile_no.unsqueeze(2).broadcast_to([P, ROUTED, NE]), ALU.is_le))
            then(dve.tensor_reduce(count[:], past[:], AX.X, ALU.add))
            then(dve.memset(tile_expert[:], 0.0))
            then(dve.tensor_scalar(tile_expert[:, SHARED_HALF:SHARED_HALF + ROUTED], count[:], float(NE - 1), 1.0,
                                   ALU.min, ALU.add))


def expert_tiles(nc, stage, x_tiles, y_tiles, x_tok, slot, tile_expert, ident, experts, tables, prefilled,
                 w_loaded, scattered):
    NT = B * QT
    WT = FF // P
    with ExitStack() as stack:
        m = Memory(nc, stack, stage)
        numbers = m.sb("numbers", [P, P])
        part_no = numbers[:, 0:1]
        row = [m.sb(f"row{i}", [P, 1], U32) for i in range(2)]
        gate = m.sb("gate", [P, 1])
        w_in = m.sb("w_in", [P, WROW])
        w_hi = [m.sb(f"w_hi{i}", [P, WROW], F32R) for i in range(2)]
        w_lo = [m.sb(f"w_lo{i}", [P, WROW], F32R) for i in range(2)]
        x_t = [m.sb(f"x_t{i}", [P, TQ, D]) for i in range(2)]
        x_hi, x_lo = m.sb("x_hi", [P, KT, TILE], F32R), m.sb("x_lo", [P, KT, TILE], F32R)
        silu = [m.sb(f"silu{i}", [P, TILE]) for i in range(2)]
        h = [m.sb(f"h{i}", [P, TILE]) for i in range(2)]
        h_hi = [m.sb(f"h_hi{i}", [P, TILE], F32R) for i in range(2)]
        h_lo = [m.sb(f"h_lo{i}", [P, TILE], F32R) for i in range(2)]
        y = [m.sb(f"y{i}", [P, TQ, D]) for i in range(2)]
        xT_ps = [m.ps(f"xT_ps{k}") for k in range(KT)]
        g_ps = [m.ps(f"g_ps{i}") for i in range(2)]
        u_ps = [m.ps(f"u_ps{i}") for i in range(2)]
        y_ps = [m.ps(f"y_ps{i}") for i in range(2)]

        loaded = m.sem("loaded")
        row_ready, gate_set = m.sem("row_ready"), m.sem("gate_set")
        whi_ready, wlo_ready = m.sem("whi_ready"), m.sem("wlo_ready")
        x_loaded, stored = m.sems("x_loaded"), m.sems("stored")
        xT_done, xhi_ready, xlo_ready = m.sem("xT_done"), m.sem("xhi_ready"), m.sem("xlo_ready")
        gu_done, silu_ready, h_ready = m.sem("gu_done"), m.sem("silu_ready"), m.sem("h_ready")
        hhi_ready, hlo_ready, down_done = m.sem("hhi_ready"), m.sem("hlo_ready"), m.sem("down_done")
        y_kept = m.sem("y_kept")
        x_rows = x_tiles.rearrange("(i q p) d -> i p q d", q=TQ, p=P)
        y_rows = y_tiles.rearrange("(i q p) d -> i p q d", q=TQ, p=P)
        LO_POOL = WROW // 2

        run = lambda eng, body: batches(eng, body, -1, ALL_TILES, 4, 4, ALL_TILES)
        block = m.block()

        def gate_cols(t, k, f):
            return t[:, k * FF + f * P:k * FF + (f + 1) * P]

        def up_cols(t, k, f):
            return t[:, (KT + k) * FF + f * P:(KT + k) * FF + (f + 1) * P]

        def down_cols(t, f):
            return t[:, 2 * KT * FF + f * D:2 * KT * FF + (f + 1) * D]

        @block.sync
        def _(sp):
            sp.dma_start(numbers[:], tables[:, 3 * P:4 * P]).then_inc(loaded, 16)
            sp.dma_start(x_t[0][:], x_rows[0]).then_inc(x_loaded[0], 16)

            def body(st):
                if st.has(2):
                    if st.has(0):
                        sp.wait_ge(xT_done, st.done(0))
                    if isinstance(st.j, int) and st.at(2) == SHARED_HALF:
                        sp.wait_ge(scattered, TOP * NT * 16)
                    sp.dma_start(x_t[st.parity(2)][:], x_rows[st.at(2)]).then_inc(x_loaded[st.parity(2)], 16)
                if st.has(-1):
                    p = st.parity(-1)
                    sp.wait_ge(y_kept, 2 * st.done(-1))
                    sp.dma_start(y_rows[st.at(-1)], y[p][:]).then_inc(stored[p], 16)

            run(sp, body)
            for p in range(2):
                sp.wait_ge(stored[p], (ALL_TILES + 1 - p) // 2 * 16)

        @block.tensor
        def _(pe):
            def transpose_x(st):
                p = st.parity(1)
                pe.wait_ge(x_loaded[p], (st.nth(1) + 1) * 16)
                if st.has(0):
                    pe.wait_ge(xlo_ready, st.done(0))
                for k in range(KT):
                    for q in range(TQ):
                        last = pe.transpose(xT_ps[k][:, q * P:(q + 1) * P], x_t[p][:, q, k * P:(k + 1) * P],
                                            ident[:])
                last.then_inc(xT_done, 1)

            def expand(st, f):
                p, n = st.parity(0), st.at(0) * WT + f
                if f == 0:
                    for sem in (xhi_ready, xlo_ready, whi_ready):
                        pe.wait_ge(sem, st.done(0))
                    pe.wait_ge(wlo_ready, 2 * st.done(0))
                if f >= 2 or st.has(-1):
                    pe.wait_ge(h_ready, n - 1)
                for bank, cols in ((g_ps[f % 2], gate_cols), (u_ps[f % 2], up_cols)):
                    for k in range(KT):
                        last = product3(pe, bank[:], (cols(w_hi[p], k, f), cols(w_lo[p], k, f)),
                                        (x_hi[:, k, :], x_lo[:, k, :]), k == 0, k == KT - 1)
                    last.then_inc(gu_done, 1)

            def contract(st, d, f):
                p, n = st.parity(d), st.at(d) * WT + f
                pe.wait_ge(hhi_ready, n + 1)
                pe.wait_ge(hlo_ready, n + 1)
                if f == 0 and st.has(d - 1):
                    pe.wait_ge(y_kept, 2 * st.done(d - 1))
                for q in range(TQ):
                    cols = slice(q * P, (q + 1) * P)
                    last = product3(pe, y_ps[q // 2][:, (q % 2) * D:(q % 2 + 1) * D],
                                    (h_hi[f % 2][:, cols], h_lo[f % 2][:, cols]),
                                    (down_cols(w_hi[p], f), down_cols(w_lo[p], f)),
                                    f == 0 and q % 2 == 0, f == WT - 1, skip_group_check=True)
                last.then_inc(down_done, 1)

            def body(st):
                for f in range(WT):
                    if st.has(0):
                        expand(st, f)
                    if f == 0 and st.has(-1):
                        contract(st, -1, WT - 1)
                    if f > 0 and st.has(0):
                        contract(st, 0, f - 1)
                    if f == 1 and st.has(1):
                        transpose_x(st)

            run(pe, body)

        def h_free(eng, st, n, f):
            if f >= 2 or st.has(-1):
                eng.wait_ge(down_done, n - 1)

        @block.scalar
        def _(act):
            def body(st):
                for f in range(WT):
                    if st.has(0):
                        n = st.at(0) * WT + f
                        act.wait_ge(gu_done, 2 * n + 1)
                        if f >= 2 or st.has(-1):
                            act.wait_ge(h_ready, n - 1)
                        nc.scalar.activation(silu[f % 2][:], g_ps[f % 2][:], ACT.Silu).then_inc(silu_ready, 1)
                        act.wait_ge(h_ready, n + 1)
                        h_free(act, st, n, f)
                        nc.scalar.activation(h_hi[f % 2][:], h[f % 2][:], ACT.Identity).then_inc(hhi_ready, 1)
                    if f == 1 and st.has(1):
                        p = st.parity(1)
                        act.wait_ge(w_loaded, st.done(1) * 16)
                        if st.has(-1):
                            act.wait_ge(down_done, st.done(-1) * WT)
                        nc.scalar.activation(w_hi[p][:], w_in[:], ACT.Identity).then_inc(whi_ready, 1)
                    if f == 3 and st.has(1):
                        act.wait_ge(xT_done, st.done(1))
                        if st.has(0):
                            act.wait_ge(gu_done, 2 * WT * st.done(0))
                        for k in range(KT):
                            last = nc.scalar.activation(x_hi[:, k, :], xT_ps[k][:], ACT.Identity)
                        last.then_inc(xhi_ready, 1)

            run(act, body)

        @block.vector
        def _(dve):
            dve.wait_ge(loaded, 16)

            def body(st):
                if st.has(1):
                    p = st.parity(1)
                    if st.has(-1):
                        dve.wait_ge(w_loaded, st.done(-1) * 16)
                    dve.tensor_scalar(row[p][:], tile_expert[:, at(st, 1)], float(P), part_no,
                                      ALU.mult, ALU.add).then_inc(row_ready, 1)
                for f in range(WT):
                    if st.has(0):
                        n = st.at(0) * WT + f
                        dve.wait_ge(gu_done, 2 * n + 2)
                        dve.wait_ge(silu_ready, n + 1)
                        if f >= 2 or st.has(-1):
                            dve.wait_ge(hhi_ready, n - 1)
                            dve.wait_ge(hlo_ready, n - 1)
                        dve.tensor_tensor(h[f % 2][:], u_ps[f % 2][:], silu[f % 2][:], ALU.mult).then_inc(h_ready, 1)
                    if f == 0 and st.has(-1):
                        p = st.parity(-1)
                        dve.wait_ge(down_done, st.done(-1) * WT)
                        if st.has(-3):
                            dve.wait_ge(stored[p], st.nth(-1) * 16)
                        for i in range(2):
                            dve.tensor_copy(y[p][:, 2 * i:2 * i + 2, :],
                                            y_ps[i][:].rearrange("p (q d) -> p q d", d=D)).then_inc(y_kept, 1)
                    if f == 2 and st.has(1):
                        p = st.parity(1)
                        dve.wait_ge(whi_ready, st.done(1))
                        if st.has(-1):
                            dve.wait_ge(down_done, st.done(-1) * WT)
                        dve.tensor_tensor(w_lo[p][:, LO_POOL:], w_in[:, LO_POOL:], w_hi[p][:, LO_POOL:].bitcast(F32),
                                          ALU.subtract).then_inc(wlo_ready, 1)
                    if f == 3 and st.has(1):
                        dve.wait_ge(xhi_ready, st.done(1))
                        if st.has(0):
                            dve.wait_ge(gu_done, 2 * WT * st.done(0))
                        for k in range(KT):
                            last = dve.tensor_tensor(x_lo[:, k, :], xT_ps[k][:], x_hi[:, k, :].bitcast(F32),
                                                     ALU.subtract)
                        last.then_inc(xlo_ready, 1)

            def at(st, d):
                return bass.ds(st.at(d), 1)

            run(dve, body)

        @block.gpsimd
        def _(pool):
            pool.wait_ge(prefilled, 16)
            n_scatter = TOP * NT // (SHARED_HALF)

            def body(st):
                if st.has(1):
                    if st.has(0):
                        pool.wait_ge(wlo_ready, 2 * st.done(0))
                        pool.wait_ge(gate_set, st.done(0))
                    pool.wait_ge(row_ready, st.done(1))
                    pool.tensor_tensor(gate[:], part_no, part_no, ALU.add).then_inc(gate_set, 1)
                    pool.indirect_dma_start(w_in[:], None, experts,
                                            bass.IndirectOffsetOnAxis(ap=row[st.parity(1)][:], axis=0)
                                            ).then_inc(w_loaded, 16)
                if isinstance(st.j, int) and st.at(0) < SHARED_HALF - 1:
                    for i in range((st.at(0) + 1) * n_scatter, (st.at(0) + 2) * n_scatter):
                        k, c = i % TOP, i // TOP
                        pool.indirect_dma_start(x_tiles, bass.IndirectOffsetOnAxis(ap=slot[k][:, c:c + 1], axis=0),
                                                x_tok[:, c, :], None).then_inc(scattered, 16)
                for f in range(WT):
                    if st.has(0):
                        n = st.at(0) * WT + f
                        pool.wait_ge(hhi_ready, n + 1)
                        h_free(pool, st, n, f)
                        pool.tensor_tensor(h_lo[f % 2][:], h[f % 2][:], h_hi[f % 2][:].bitcast(F32),
                                           ALU.subtract).then_inc(hlo_ready, 1)
                    if f == 2 and st.has(1):
                        p = st.parity(1)
                        pool.wait_ge(whi_ready, st.done(1))
                        if st.has(-1):
                            pool.wait_ge(down_done, st.done(-1) * WT)
                        pool.tensor_tensor(w_lo[p][:, 0:LO_POOL], w_in[:, 0:LO_POOL],
                                           w_hi[p][:, 0:LO_POOL].bitcast(F32), ALU.subtract).then_inc(wlo_ready, 1)

            run(pool, body)


def combine(nc, stage, x_in, x_out, y_tiles, slot, weight, routed_loaded):
    with ExitStack() as stack:
        m = Memory(nc, stack, stage)
        y_shared = [m.sb(f"y_shared{i}", [P, QT, D]) for i in range(2)]
        y_routed = [m.sb(f"y_routed{i}", [P, TOP, QT, D]) for i in range(2)]
        part = m.sb("part", [P, TOP, QT, D])
        sh_loaded = m.sems("sh_loaded")
        part_ready, sum_ready = m.sem("part_ready"), m.sem("sum_ready")
        norm = RowNorm(m, x_in, x_out, sum_ready)
        half = B * S // 2
        row0 = lambda b: b * S if b < B // 2 else b * S + ROUTED * TILE
        block = m.block()

        @block.sync
        def _(sp):
            for b in range(-1, B):
                st = Step(0, b)
                if st.has(1):
                    p, r0 = st.parity(1), row0(b + 1)
                    norm.load(sp, st, 1)
                    if st.has(-1):
                        sp.wait_ge(part_ready, 4 * st.done(-1))
                    sp.dma_start(y_shared[p][:], y_tiles[r0:r0 + S, :].rearrange("(q p) d -> p q d", p=P)
                                 ).then_inc(sh_loaded[p], 16)
                if st.has(0):
                    norm.store(sp, st, 0)
            norm.all_stored(sp)

        @block.gpsimd
        def _(pool):
            norm.constants(pool)
            for b in range(-1, B):
                st = Step(0, b)
                if st.has(1):
                    p = st.parity(1)
                    if st.has(-1):
                        pool.wait_ge(sum_ready, st.done(-1))
                    for k in range(TOP):
                        for q in range(QT):
                            c = (b + 1) * QT + q
                            pool.indirect_dma_start(y_routed[p][:, k, q, :], None, y_tiles,
                                                    bass.IndirectOffsetOnAxis(ap=slot[k][:, c:c + 1], axis=0)
                                                    ).then_inc(routed_loaded[p], 16)
                if st.has(0):
                    norm.inverse_root(pool, st, 0)

        @block.vector
        def _(dve):
            for b in range(B):
                st = Step(0, b)
                p, n = st.parity(0), st.done(0)
                dve.wait_ge(sh_loaded[p], (st.nth(0) + 1) * 16)
                dve.wait_ge(routed_loaded[p], (st.nth(0) + 1) * TOP * QT * 16)
                for k in range(TOP):
                    if k:
                        dve.wait_ge(part_ready, 4 * (n - 1) + 2)
                    elif b:
                        dve.wait_ge(norm.r_ready, n - 1)
                    for q in range(QT):
                        c = b * QT + q
                        before = y_shared[p][:, q, :] if k == 0 else part[:, 0, q, :]
                        last = dve.scalar_tensor_tensor(part[:, k, q, :], y_routed[p][:, k, q, :],
                                                        weight[k][:, c:c + 1], before, ALU.mult, ALU.add)
                        last.then_inc(part_ready, 1)
                dve.wait_ge(part_ready, 4 * n)
                dve.memset(norm.gate[:], 0.0).then_inc(sum_ready, 1)
                norm.residual(dve, st, 0, [part[:, 1, q, :] for q in range(QT)])
                norm.finish(dve, st, 0)


def state_space(nc, stage, x_in, x_out, w_in, conv_w, conv_b, norm_w, w_out, dt_bias, a_log, d_cols, tri, consts):
    N_IN, NH, HP, FT = 1288, 8, 64, 4
    INNER = FT * P
    DT0 = N_IN - NH
    UNITS = 6
    with ExitStack() as stack:
        m = Memory(nc, stack, stage)
        w_all = m.sb("w_all", [P, KT, N_IN])
        w_hi, w_lo = m.sb("w_hi", [P, KT, N_IN], F32R), m.sb("w_lo", [P, KT, N_IN], F32R)
        wo_in, wo_full = m.sb("wo_in", [P, FT, D]), m.sb("wo_full", [P, FT, D])
        wo_hi, wo_lo = m.sb("wo_hi", [P, FT, D], F32R), m.sb("wo_lo", [P, FT, D], F32R)
        cw, cb = m.sb("cw", [P, 6, 4]), m.sb("cb", [P, 6])
        nw, dcol = m.sb("nw", [P, FT]), m.sb("dcol", [P, FT])
        bias, alog, aexp, aneg = (m.sb("bias", [P, NH]), m.sb("alog", [P, NH]), m.sb("aexp", [P, NH]),
                                  m.sb("aneg", [P, NH]))
        ident = m.sb("ident", [P, P])
        triang = m.sb("triang", [P, 5, P])
        upto, gmask = triang[:, 0, :], triang[:, 0:3, :]
        after, one_r = m.sb("after", [P, P], F32R), m.sb("one_r", [P, P], F32R)
        x_tok = [m.sb(f"x_tok{i}", [P, QT, D]) for i in range(2)]
        x_hi, x_lo = m.sb("x_hi", [P, KT, S], F32R), m.sb("x_lo", [P, KT, S], F32R)
        conv = [m.sb(f"conv{u}", [P, 2, S]) for u in range(3)]
        bc = [m.sb(f"bc{i}", [P, 2, S]) for i in range(2)]
        xs = [m.sb(f"xs{i}", [P, FT, S]) for i in range(2)]
        zs = [m.sb(f"zs{i}", [P, FT, S]) for i in range(2)]
        v, v_abs, e_v, ln_v, dt, a = (m.sb(n, [P, QT, NH]) for n in ("v", "v_abs", "e_v", "ln_v", "dt", "a"))
        a_hi, a_lo = m.sb("a_hi", [P, QT, NH], F32R), m.sb("a_lo", [P, QT, NH], F32R)
        rhs_hi, rhs_lo = m.sb("rhs_hi", [P, QT, NH, P], F32R), m.sb("rhs_lo", [P, QT, NH, P], F32R)
        tail = m.sb("tail", [P, NH])
        gm = m.sb("gm", [P, 3, P])
        decay = m.sb("decay", [P, 6, 4, P])
        mat = m.sb("mat", [P, 6, 4, P])
        xdt = m.sb("xdt", [P, QT, INNER])
        xdt_tail = m.sb("xdt_tail", [P, INNER])
        yd, yz = m.sb("yd", [P, FT, S]), m.sb("yz", [P, FT, S])
        y_hi, y_lo = m.sb("y_hi", [P, FT, S], F32R), m.sb("y_lo", [P, FT, S], F32R)
        square = m.sb("square", [P, FT, S])
        ms, row_scale = m.sb("ms", [P, QT]), m.sb("row_scale", [P, QT])

        xT_ps, g_ps = m.ps("xT_ps"), m.ps("g_ps")
        in_ps = [m.ps(f"in_ps{i}") for i in range(2)]
        e_ps = [m.ps(f"e_ps{i}") for i in range(2)]
        y_ps = [m.ps(f"y_ps{i}") for i in range(2)]

        loaded, ready, lo_ready = m.sem("loaded"), m.sem("ready"), m.sem("lo_ready")
        aexp_ready, wo_ready = m.sem("aexp_ready"), m.sem("wo_ready")
        x_loaded, xT_done, xhi_ready, xlo_ready = (m.sems("x_loaded"), m.sem("xT_done"), m.sem("xhi_ready"),
                                                   m.sem("xlo_ready"))
        in_done, tap_ready, conv_ready = m.sem("in_done"), m.sem("tap_ready"), m.sem("conv_ready")
        last_tap = m.sem("last_tap")
        silu_ready, z_ready = m.sem("silu_ready"), m.sem("z_ready")
        v_ready, abs_ready, ev_ready, ln_ready = m.sem("v_ready"), m.sem("abs_ready"), m.sem("ev_ready"), m.sem("ln_ready")
        dt_ready, a_ready, ahi_ready, alo_ready = m.sem("dt_ready"), m.sem("a_ready"), m.sem("ahi_ready"), m.sem("alo_ready")
        rhi_ready, rlo_ready = m.sem("rhi_ready"), m.sem("rlo_ready")
        g_done, gm_ready, tail_ready = m.sem("g_done"), m.sem("gm_ready"), m.sem("tail_ready")
        e_done, decay_ready, mat_ready = m.sem("e_done"), m.sem("decay_ready"), m.sem("mat_ready")
        rows_done, xdt_ready, xtail_ready = m.sem("rows_done"), m.sem("xdt_ready"), m.sem("xtail_ready")
        ssm_done, yd_ready, yz_ready = m.sem("ssm_done"), m.sem("yd_ready"), m.sem("yz_ready")
        yhi_ready, ylo_ready, sq_ready = m.sem("yhi_ready"), m.sem("ylo_ready"), m.sem("sq_ready")
        ssq_done, ms_ready, scale_ready, y_done = m.sem("ssq_done"), m.sem("ms_ready"), m.sem("scale_ready"), m.sem("y_done")
        norm = RowNorm(m, x_in, x_out, y_done)
        x_rows = x_in.rearrange("(b q p) d -> b p q d", q=QT, p=P)
        LOADS = 10

        run = lambda eng, body: batches(eng, body, -1, B, 4, 4)
        block = m.block()

        @block.sync
        def _(sp):
            for dst, src in ((w_all, w_in), (wo_in, w_out), (cw, conv_w), (cb, conv_b), (nw, norm_w),
                             (dcol, d_cols), (ident, consts["ident"]), (triang, tri)):
                sp.dma_start(dst[:], src).then_inc(loaded, 16)
            sp.dma_start(bias[:], dt_bias.partition_broadcast(P)).then_inc(loaded, 16)
            sp.dma_start(alog[:], a_log.partition_broadcast(P)).then_inc(loaded, 16)
            sp.dma_start(x_tok[0][:], x_rows[0]).then_inc(x_loaded[0], 16)

            def body(st):
                if st.has(2):
                    if st.has(0):
                        sp.wait_ge(xT_done, st.done(0))
                    sp.dma_start(x_tok[st.parity(2)][:], x_rows[st.at(2)]).then_inc(x_loaded[st.parity(2)], 16)
                if st.has(-1):
                    norm.load(sp, st, -1)
                    norm.store(sp, st, -1)

            run(sp, body)
            norm.all_stored(sp)

        @block.tensor
        def _(pe):
            pe.wait_ge(loaded, LOADS * 16)
            pe.wait_ge(ready, 3)
            pe.wait_ge(lo_ready, 2)

            def transpose_x(st):
                p = st.parity(1)
                pe.wait_ge(x_loaded[p], (st.nth(1) + 1) * 16)
                if st.has(0):
                    pe.wait_ge(xlo_ready, st.done(0))
                for k in range(KT):
                    for q in range(QT):
                        last = pe.transpose(xT_ps[:, k * S + q * P:k * S + (q + 1) * P],
                                            x_tok[p][:, q, k * P:(k + 1) * P], ident[:])
                last.then_inc(xT_done, 1)

            def state_products(st):
                n, p = st.done(0), st.parity(0)
                pe.wait_ge(silu_ready, 3 * n - 2)
                if st.has(-1):
                    pe.wait_ge(ms_ready, n - 1)
                pe.wait_ge(ahi_ready, n)
                pe.wait_ge(alo_ready, n)
                pe.matmul(g_ps[:, S + P:S + P + NH], after[:], a_hi[:, 0, :], start=True, stop=False)
                pe.matmul(g_ps[:, S + P:S + P + NH], after[:], a_lo[:, 0, :], start=False, stop=True)
                pe.matmul(g_ps[:, 0:S], bc[p][:, 0, 0:P], bc[p][:, 1, :], start=True, stop=True)
                pe.matmul(g_ps[:, S:S + P], bc[p][:, 0, P:S], bc[p][:, 1, P:S],
                          start=True, stop=True).then_inc(g_done, 1)

            def exponents(st, u):
                blk, h0 = u // 2, 4 * (u % 2)
                n = st.done(0)
                if u == 0:
                    pe.wait_ge(rhi_ready, n)
                    pe.wait_ge(rlo_ready, n)
                if u >= 2:
                    pe.wait_ge(decay_ready, st.at(0) * 6 + u - 1)
                else:
                    pe.wait_ge(xdt_ready, 2 * n - 1 + u)
                lhs, q = (after, one_r, after)[blk], (0, 1, 1)[blk]
                out = e_ps[u % 2][:]
                pe.matmul(out, lhs[:], rhs_hi[:, q, h0:h0 + 4, :], start=True, stop=False)
                pe.matmul(out, lhs[:], rhs_lo[:, q, h0:h0 + 4, :], start=False, stop=True).then_inc(e_done, 1)

            def project(st, u):
                n, k0 = st.at(1), st.done(1)
                if u == 0:
                    pe.wait_ge(xhi_ready, k0)
                    pe.wait_ge(xlo_ready, k0)
                if u < 2:
                    if st.has(0):
                        pe.wait_ge(z_ready, 2 * n - 1 + u)
                elif u < 5:
                    pe.wait_ge(conv_ready, 3 * n + u - 1)
                else:
                    pe.wait_ge(v_ready, k0)
                bank = in_ps[u % 2]
                if u == 3:
                    for q in range(QT):
                        for k in range(KT):
                            cols = slice(q * P, (q + 1) * P)
                            last = product3(pe, bank[:, q * NH:(q + 1) * NH],
                                            (x_hi[:, k, cols], x_lo[:, k, cols]),
                                            (w_hi[:, k, DT0:N_IN], w_lo[:, k, DT0:N_IN]), k == 0, k == KT - 1)
                else:
                    first = {0: 8, 1: 4, 2: 6, 4: 0, 5: 2}[u]
                    for j in range(2):
                        cols = slice((first + j) * P, (first + j + 1) * P)
                        for k in range(KT):
                            last = product3(pe, bank[:, j * S:(j + 1) * S],
                                            (w_hi[:, k, cols], w_lo[:, k, cols]),
                                            (x_hi[:, k, :], x_lo[:, k, :]), k == 0, k == KT - 1)
                last.then_inc(in_done, 1)

            def mix(st, b):
                n = st.done(0)
                if b == 0:
                    pe.wait_ge(xtail_ready, n)
                    if st.has(-1):
                        pe.wait_ge(norm.r_ready, n - 1)
                elif st.has(-1):
                    pe.wait_ge(yd_ready, 2 * (n - 1))
                pe.wait_ge(mat_ready, 6 * n - 1 + b)
                for f in range(2):
                    for half in range(2):
                        h = 4 * b + 2 * f + half
                        rows, cols = slice(half * HP, (half + 1) * HP), slice(h * HP, (h + 1) * HP)
                        out = y_ps[b][rows, f * S:(f + 1) * S]
                        kw = dict(skip_group_check=True)
                        pe.matmul(out[:, P:S], xdt_tail[:, cols], mat[:, 2 + b, h % 4, :], start=True, stop=False, **kw)
                        pe.matmul(out[:, P:S], xdt[:, 1, cols], mat[:, 4 + b, h % 4, :], start=False, stop=True, **kw)
                        last = pe.matmul(out[:, 0:P], xdt[:, 0, cols], mat[:, b, h % 4, :], start=True, stop=True, **kw)
                last.then_inc(ssm_done, 1)

            def to_rows(st, q):
                n, p = st.done(1), st.parity(1)
                pe.wait_ge(silu_ready, 3 * n)
                if st.has(0):
                    pe.wait_ge(decay_ready, 6 * st.done(0) - 1 + q)
                for f in range(FT):
                    last = pe.transpose(e_ps[q][:, f * P:(f + 1) * P], xs[p][:, f, q * P:(q + 1) * P], ident[:])
                last.then_inc(rows_done, 1)

            def output(st):
                n = st.done(0)
                pe.wait_ge(sq_ready, n)
                pe.wait_ge(tail_ready, n)
                pe.wait_ge(gm_ready, n)
                for q in range(QT):
                    for f in range(FT):
                        last = pe.matmul(g_ps[:, q:q + 1], square[:, f, q * P:(q + 1) * P], triang[:, 1, 0:1],
                                         start=f == 0, stop=f == FT - 1)
                last.then_inc(ssq_done, 1)
                pe.wait_ge(yhi_ready, n)
                pe.wait_ge(ylo_ready, n)
                pe.wait_ge(yd_ready, 2 * n)
                for q in range(QT):
                    cols = slice(q * P, (q + 1) * P)
                    for f in range(FT):
                        last = product3(pe, y_ps[0][:, q * D:(q + 1) * D], (y_hi[:, f, cols], y_lo[:, f, cols]),
                                        (wo_hi[:, f, :], wo_lo[:, f, :]), f == 0, f == FT - 1)
                last.then_inc(y_done, 1)

            def body(st):
                now, nxt = st.has(0), st.has(1)
                if nxt:
                    transpose_x(st)
                if now:
                    state_products(st)
                for u in range(3):
                    if now:
                        exponents(st, 2 * u)
                        exponents(st, 2 * u + 1)
                    if nxt:
                        project(st, u)
                if nxt:
                    project(st, 3)
                    project(st, 4)
                if now:
                    mix(st, 0)
                    mix(st, 1)
                if nxt:
                    project(st, 5)
                    to_rows(st, 0)
                    to_rows(st, 1)
                if now:
                    output(st)

            run(pe, body)

        @block.scalar
        def _(act):
            act.wait_ge(loaded, LOADS * 16)
            nc.scalar.activation(aexp[:], alog[:], ACT.Exp).then_inc(aexp_ready, 1)

            def decays(st, u):
                act.wait_ge(e_done, st.at(0) * 6 + u + 1)
                if u == 0 and st.has(-1):
                    act.wait_ge(mat_ready, 6 * st.done(-1))
                nc.scalar.activation(decay[:, u, :, :].rearrange("p h t -> p (h t)"), e_ps[u % 2][:],
                                     ACT.Exp).then_inc(decay_ready, 1)

            def first_tap(st, u):
                n, first = st.at(1), (4, 0, 2)[u]
                act.wait_ge(in_done, n * UNITS + u + 1)
                if st.has(0):
                    act.wait_ge(silu_ready, 3 * n)
                for j in range(2):
                    last = nc.scalar.activation(conv[u][:, j, :], in_ps[u % 2][:, j * S:(j + 1) * S], ACT.Identity,
                                                bias=cb[:, first + j:first + j + 1],
                                                scale=cw[:, first + j, 3:4])
                last.then_inc(tap_ready, 1)

            def body(st):
                now, nxt = st.has(0), st.has(1)
                if nxt:
                    act.wait_ge(xT_done, st.done(1))
                    if now:
                        act.wait_ge(in_done, UNITS * st.at(1))
                    nc.scalar.activation(x_hi[:].rearrange("p k s -> p (k s)"), xT_ps[:],
                                         ACT.Identity).then_inc(xhi_ready, 1)
                if now:
                    act.wait_ge(gm_ready, st.done(0))
                    if st.has(-1):
                        act.wait_ge(xtail_ready, st.done(-1))
                    nc.scalar.activation(tail[:], g_ps[:, S + P:S + P + NH], ACT.Exp).then_inc(tail_ready, 1)
                for u in range(3):
                    if now:
                        decays(st, 2 * u)
                        decays(st, 2 * u + 1)
                    if nxt:
                        first_tap(st, u)
                if nxt:
                    n, p = st.done(1), st.parity(1)
                    act.wait_ge(v_ready, n)
                    if now:
                        act.wait_ge(dt_ready, n - 1)
                    nc.scalar.activation(v_abs[:], v[:], ACT.Abs).then_inc(abs_ready, 1)
                    act.wait_ge(abs_ready, n)
                    nc.scalar.activation(e_v[:], v_abs[:], ACT.Exp, scale=-1.0).then_inc(ev_ready, 1)
                    act.wait_ge(ev_ready, n)
                    nc.scalar.activation(ln_v[:], e_v[:], ACT.Ln, bias=triang[:, 1, 0:1]).then_inc(ln_ready, 1)
                    for u in range(3):
                        act.wait_ge(conv_ready, 3 * st.at(1) + u + 1)
                        if u == 0 and st.has(-1):
                            act.wait_ge(yd_ready, 2 * st.done(-1))
                        dst = bc[p][:] if u == 0 else xs[p][:, 2 * u - 2:2 * u, :]
                        nc.scalar.activation(dst.rearrange("p j s -> p (j s)"), conv[u][:].rearrange("p j s -> p (j s)"),
                                             ACT.Silu).then_inc(silu_ready, 1)
                    for u in range(2):
                        act.wait_ge(in_done, st.at(1) * UNITS + 5 + u)
                        if u == 0 and st.has(-1):
                            act.wait_ge(yz_ready, st.done(-1))
                        nc.scalar.activation(zs[p][:, 2 * u:2 * u + 2, :].rearrange("p j s -> p (j s)"), in_ps[u][:],
                                             ACT.Silu).then_inc(z_ready, 1)
                if now:
                    n = st.done(0)
                    act.wait_ge(yz_ready, n)
                    if st.has(-1):
                        act.wait_ge(ssq_done, n - 1)
                        act.wait_ge(y_done, n - 1)
                    nc.scalar.activation(y_hi[:].rearrange("p f s -> p (f s)"), yz[:].rearrange("p f s -> p (f s)"),
                                         ACT.Identity).then_inc(yhi_ready, 1)
                    nc.scalar.activation(square[:].rearrange("p f s -> p (f s)"), yz[:].rearrange("p f s -> p (f s)"),
                                         ACT.Square).then_inc(sq_ready, 1)

            run(act, body)

        @block.vector
        def _(dve):
            dve.wait_ge(loaded, LOADS * 16)
            dve.tensor_copy(w_hi[:], w_all[:]).then_inc(ready, 1)
            dve.tensor_copy(after[:], triang[:, 3, :]).then_inc(ready, 1)
            dve.tensor_copy(one_r[:], triang[:, 4, :]).then_inc(ready, 1)
            for f in range(FT):
                last = dve.tensor_scalar(wo_full[:, f, :], wo_in[:, f, :], nw[:, f:f + 1], None, ALU.mult)
            last.then_inc(wo_ready, 1)
            dve.wait_ge(wo_ready, 1)
            dve.tensor_copy(wo_hi[:], wo_full[:]).then_inc(wo_ready, 1)
            dve.wait_ge(aexp_ready, 1)
            dve.tensor_scalar(aneg[:], aexp[:], -1.0, None, ALU.mult).then_inc(aexp_ready, 1)
            dve.wait_ge(aexp_ready, 2)

            def matrices(st, u):
                dve.wait_ge(decay_ready, st.at(0) * 6 + u + 1)
                if u == 0 and st.has(-1):
                    dve.wait_ge(ssm_done, 2 * st.done(-1))
                dve.tensor_tensor(mat[:, u, :, :], decay[:, u, :, :],
                                  gm[:, u // 2, :].unsqueeze(1).broadcast_to([P, 4, P]),
                                  ALU.mult).then_inc(mat_ready, 1)

            def taps(st, u):
                n, first = st.at(1), (4, 0, 2)[u]
                dve.wait_ge(tap_ready, 3 * n + u + 1)
                for back in range(1, 4):
                    if back > 1:
                        dve.wait_ge(last_tap, 6 * n + 2 * u + back - 1)
                    for j in range(2):
                        last = dve.scalar_tensor_tensor(
                            conv[u][:, j, back:S], in_ps[u % 2][:, j * S:(j + 1) * S - back],
                            cw[:, first + j, 3 - back:4 - back], conv[u][:, j, back:S], ALU.mult, ALU.add)
                    last.then_inc(last_tap if back < 3 else conv_ready, 1)

            def heads(ap):
                return ap.rearrange("p (h e) -> p h e", e=HP)

            def spread(ap):
                return ap.unsqueeze(2).broadcast_to([P, NH, HP])

            def body(st):
                now, nxt = st.has(0), st.has(1)
                p, pn, n, nn = st.parity(0), st.parity(1), st.done(0), st.done(1)
                if nxt:
                    dve.wait_ge(xhi_ready, nn)
                    if now:
                        dve.wait_ge(in_done, UNITS * st.at(1))
                    dve.tensor_tensor(x_lo[:].rearrange("p k s -> p (k s)"), xT_ps[:],
                                      x_hi[:].bitcast(F32).rearrange("p k s -> p (k s)"),
                                      ALU.subtract).then_inc(xlo_ready, 1)
                if now:
                    dve.wait_ge(g_done, n)
                    if st.has(-1):
                        dve.wait_ge(mat_ready, 6 * (n - 1))
                    dve.tensor_tensor(gm[:], g_ps[:, 0:S + P].rearrange("p (b t) -> p b t", t=P), gmask,
                                      ALU.mult).then_inc(gm_ready, 1)
                    dve.wait_ge(tail_ready, n)
                    dve.wait_ge(xdt_ready, 2 * n)
                    if st.has(-1):
                        dve.wait_ge(ssm_done, 2 * (n - 1))
                    dve.tensor_tensor(heads(xdt_tail[:]), heads(xdt[:, 0, :]), spread(tail[:]),
                                      ALU.mult).then_inc(xtail_ready, 1)
                    dve.wait_ge(gm_ready, n)
                if st.has(-1):
                    dve.wait_ge(scale_ready, st.done(-1))
                    norm.residual(dve, st, -1, [y_ps[0][:, q * D:(q + 1) * D] for q in range(QT)], row_scale)
                for u in range(3):
                    if now:
                        matrices(st, 2 * u)
                        matrices(st, 2 * u + 1)
                    if u == 0 and st.has(-1):
                        norm.finish(dve, st, -1)
                    if nxt:
                        taps(st, u)
                if nxt:
                    dve.wait_ge(in_done, st.at(1) * UNITS + 4)
                    if now:
                        dve.wait_ge(dt_ready, n)
                    dve.tensor_tensor(v[:], in_ps[1][:, 0:QT * NH].rearrange("p (q h) -> p q h", h=NH),
                                      bias[:].unsqueeze(1).broadcast_to([P, QT, NH]),
                                      ALU.add).then_inc(v_ready, 1)
                if now:
                    for b in range(2):
                        dve.wait_ge(ssm_done, 2 * st.at(0) + b + 1)
                        for j in range(2):
                            f = 2 * b + j
                            last = dve.scalar_tensor_tensor(yd[:, f, :], xs[p][:, f, :], dcol[:, f:f + 1],
                                                            y_ps[b][:, j * S:(j + 1) * S], ALU.mult, ALU.add)
                        last.then_inc(yd_ready, 1)
                if nxt:
                    dve.wait_ge(ln_ready, nn)
                    dve.wait_ge(v_ready, nn)
                    dve.scalar_tensor_tensor(dt[:], v[:], 0.0, ln_v[:], ALU.max, ALU.add).then_inc(dt_ready, 1)
                    dve.wait_ge(dt_ready, nn)
                    dve.tensor_tensor(a[:], dt[:], aneg[:].unsqueeze(1).broadcast_to([P, QT, NH]),
                                      ALU.mult).then_inc(a_ready, 1)
                    if now:
                        dve.wait_ge(e_done, 6 * n)
                        dve.wait_ge(g_done, n)
                        dve.wait_ge(rlo_ready, n)
                    dve.wait_ge(a_ready, nn)
                    dve.tensor_copy(a_hi[:], a[:]).then_inc(ahi_ready, 1)
                    dve.wait_ge(ahi_ready, nn)
                    dve.tensor_tensor(a_lo[:], a[:], a_hi[:].bitcast(F32), ALU.subtract).then_inc(alo_ready, 1)
                    for q in range(QT):
                        last = dve.tensor_tensor(rhs_hi[:, q, :, :], upto.unsqueeze(1).broadcast_to([P, NH, P]),
                                                 a_hi[:, q, :].bitcast(F32).unsqueeze(2).broadcast_to([P, NH, P]),
                                                 ALU.mult)
                    last.then_inc(rhi_ready, 1)
                if now:
                    dve.wait_ge(yd_ready, 2 * n)
                    dve.wait_ge(z_ready, 2 * n)
                    if st.has(-1):
                        dve.wait_ge(sq_ready, n - 1)
                        dve.wait_ge(ylo_ready, n - 1)
                    dve.tensor_tensor(yz[:], yd[:], zs[p][:], ALU.mult).then_inc(yz_ready, 1)
                if nxt:
                    if now:
                        dve.wait_ge(ssm_done, 2 * n)
                    for q in range(QT):
                        dve.wait_ge(rows_done, 2 * st.at(1) + q + 1)
                        dve.tensor_tensor(heads(xdt[:, q, :]), heads(e_ps[q][:]), spread(dt[:, q, :]),
                                          ALU.mult).then_inc(xdt_ready, 1)
                if now:
                    dve.wait_ge(ssq_done, n)
                    dve.tensor_scalar(ms[:], g_ps[:, 0:QT], 1.0 / INNER, EPS, ALU.mult, ALU.add).then_inc(ms_ready, 1)

            run(dve, body)

        @block.gpsimd
        def _(pool):
            norm.constants(pool)
            pool.wait_ge(ready, 1)
            pool.tensor_tensor(w_lo[:], w_all[:], w_hi[:].bitcast(F32), ALU.subtract).then_inc(lo_ready, 1)
            pool.wait_ge(wo_ready, 2)
            pool.tensor_tensor(wo_lo[:], wo_full[:], wo_hi[:].bitcast(F32), ALU.subtract).then_inc(lo_ready, 1)

            def body(st):
                n, nn = st.done(0), st.done(1)
                if st.has(-1):
                    norm.inverse_root(pool, st, -1)
                if st.has(1):
                    pool.wait_ge(alo_ready, nn)
                    if st.has(0):
                        pool.wait_ge(e_done, 6 * n)
                    for q in range(QT):
                        last = pool.tensor_tensor(rhs_lo[:, q, :, :], upto.unsqueeze(1).broadcast_to([P, NH, P]),
                                                  a_lo[:, q, :].bitcast(F32).unsqueeze(2).broadcast_to([P, NH, P]),
                                                  ALU.mult)
                    last.then_inc(rlo_ready, 1)
                if st.has(0):
                    pool.wait_ge(yhi_ready, n)
                    pool.tensor_tensor(y_lo[:], yz[:], y_hi[:].bitcast(F32), ALU.subtract).then_inc(ylo_ready, 1)
                    pool.wait_ge(ms_ready, n)
                    if st.has(-1):
                        pool.wait_ge(norm.r_ready, n - 1)
                    pool.tensor_tensor(row_scale[:], ms[:], norm.neg_half[:], ALU.pow).then_inc(scale_ready, 1)

            run(pool, body)


def lora_feed_forward(nc, stage, x_in, x_out, wi, wo, lora_a, lora_b, top_idx, top_val, expert_of_row, consts):
    F, FT = 1024, 8
    PAIRS = FT // 2
    with ExitStack() as stack:
        m = Memory(nc, stack, stage)
        w_in = m.sb("w_in", [P, KT, F])
        wo_in = m.sb("wo_in", [P, FT, D])
        a_in, b_in = m.sb("a_in", [P, D]), m.sb("b_in", [P, F])
        b_sel = [m.sb(f"b_sel{k}", [P, F]) for k in range(2)]
        merged = [m.sb(f"merged{k}", [P, KT, F]) for k in range(2)]
        wm_hi = [m.sb(f"wm_hi{k}", [P, KT, F], F32R) for k in range(2)]
        wm_lo = [m.sb(f"wm_lo{k}", [P, KT, F], F32R) for k in range(2)]
        wo_hi, wo_lo = m.sb("wo_hi", [P, FT, D], F32R), m.sb("wo_lo", [P, FT, D], F32R)
        idx, val = m.sb("idx", [P, 2], I32), m.sb("val", [P, 2])
        row_expert, sel = m.sb("row_expert", [P, 1]), m.sb("sel", [P, 2])
        ident = m.sb("ident", [P, P])
        x_tok = [m.sb(f"x_tok{i}", [P, QT, D]) for i in range(2)]
        x_hi = [m.sb(f"x_hi{i}", [P, KT, S], F32R) for i in range(2)]
        x_lo = [m.sb(f"x_lo{i}", [P, KT, S], F32R) for i in range(2)]
        z0 = [m.sb(f"z0_{i}", [P, 2 * S]) for i in range(2)]
        z1 = [m.sb(f"z1_{i}", [P, 2 * S]) for i in range(2)]
        g_full = [m.sb(f"g_full{i}", [P, 2 * S]) for i in range(2)]
        g_hi = [m.sb(f"g_hi{i}", [P, 2, S], F32R) for i in range(2)]
        g_lo = [m.sb(f"g_lo{i}", [P, 2, S], F32R) for i in range(2)]

        xT_ps = m.ps("xT_ps")
        z_ps = [[m.ps(f"z_ps{i}{k}") for k in range(2)] for i in range(2)]
        y_ps = [m.ps(f"y_ps{q}", (P, 512)) for q in range(QT)]

        loaded, w_ready, lo_ready = m.sem("loaded"), m.sem("w_ready"), m.sem("lo_ready")
        sel_ready, bsel_ready = m.sem("sel_ready"), m.sem("bsel_ready")
        lora_done, merged_ready = m.sem("lora_done"), m.sem("merged_ready")
        x_loaded = m.sems("x_loaded")
        xT_done, xhi_ready, xlo_ready = m.sem("xT_done"), m.sem("xhi_ready"), m.sem("xlo_ready")
        z_done, z0_ready, z1_ready, g_ready = m.sem("z_done"), m.sem("z0_ready"), m.sem("z1_ready"), m.sem("g_ready")
        ghi_ready, glo_ready, out_done, y_done = (m.sem("ghi_ready"), m.sem("glo_ready"),
                                                  m.sem("out_done"), m.sem("y_done"))
        norm = RowNorm(m, x_in, x_out, y_done)
        x_rows = x_in.rearrange("(b q p) d -> b p q d", q=QT, p=P)

        run = lambda eng, body: batches(eng, body, -1, B, 4, 4)
        block = m.block()

        @block.sync
        def _(sp):
            sp.dma_start(a_in[:], lora_a).then_inc(loaded, 16)
            sp.dma_start(b_in[:], lora_b).then_inc(loaded, 16)
            sp.dma_start(idx[:], top_idx.partition_broadcast(P)).then_inc(loaded, 16)
            sp.dma_start(val[:], top_val.partition_broadcast(P)).then_inc(loaded, 16)
            sp.dma_start(row_expert[:], expert_of_row).then_inc(loaded, 16)
            sp.dma_start(w_in[:], wi).then_inc(loaded, 16)
            sp.dma_start(wo_in[:], wo).then_inc(loaded, 16)
            sp.dma_start(ident[:], consts["ident"]).then_inc(loaded, 16)
            sp.dma_start(x_tok[0][:], x_rows[0]).then_inc(x_loaded[0], 16)

            def body(st):
                if st.has(2):
                    if st.has(0):
                        sp.wait_ge(xT_done, st.done(0))
                    sp.dma_start(x_tok[st.parity(2)][:], x_rows[st.at(2)]).then_inc(x_loaded[st.parity(2)], 16)
                if st.has(-1):
                    norm.load(sp, st, -1)
                    norm.store(sp, st, -1)

            run(sp, body)
            norm.all_stored(sp)

        @block.tensor
        def _(pe):
            pe.wait_ge(loaded, 8 * 16)
            for k in range(2):
                pe.wait_ge(bsel_ready, k + 1)
                if k:
                    pe.wait_ge(merged_ready, 4)
                for d in range(KT):
                    for f in range(2):
                        pe.matmul(z_ps[d][f][:], a_in[:, d * P:(d + 1) * P], b_sel[k][:, f * 512:(f + 1) * 512],
                                  start=True, stop=True).then_inc(lora_done, 1)
            pe.wait_ge(w_ready, 3)
            pe.wait_ge(lo_ready, 3)

            def transpose_x(st):
                p = st.parity(1)
                pe.wait_ge(x_loaded[p], (st.nth(1) + 1) * 16)
                if st.has(0):
                    pe.wait_ge(xlo_ready, st.done(0))
                for k in range(KT):
                    for q in range(QT):
                        last = pe.transpose(xT_ps[:, k * S + q * P:k * S + (q + 1) * P],
                                            x_tok[p][:, q, k * P:(k + 1) * P], ident[:])
                last.then_inc(xT_done, 1)

            def expand(st, f):
                p, n = st.parity(0), st.at(0) * PAIRS + f
                if f == 0:
                    pe.wait_ge(xhi_ready, st.done(0))
                    pe.wait_ge(xlo_ready, st.done(0))
                if f >= 2 or st.has(-1):
                    pe.wait_ge(z0_ready, n - 1)
                    pe.wait_ge(z1_ready, n - 1)
                for e in range(2):
                    for j in range(2):
                        cols = slice((2 * f + j) * P, (2 * f + j + 1) * P)
                        for k in range(KT):
                            last = product3(pe, z_ps[f % 2][e][:, j * S:(j + 1) * S],
                                            (wm_hi[e][:, k, cols], wm_lo[e][:, k, cols]),
                                            (x_hi[p][:, k, :], x_lo[p][:, k, :]), k == 0, k == KT - 1)
                    last.then_inc(z_done, 1)

            def contract(st, d, f):
                n = st.at(d) * PAIRS + f
                pe.wait_ge(ghi_ready, n + 1)
                pe.wait_ge(glo_ready, n + 1)
                if f == 0 and st.has(d - 1):
                    pe.wait_ge(norm.r_ready, st.done(d - 1))
                for q in range(QT):
                    cols = slice(q * P, (q + 1) * P)
                    for j in range(2):
                        last = product3(pe, y_ps[q][:, 0:D], (g_hi[f % 2][:, j, cols], g_lo[f % 2][:, j, cols]),
                                        (wo_hi[:, 2 * f + j, :], wo_lo[:, 2 * f + j, :]),
                                        f == 0 and j == 0, f == PAIRS - 1 and j == 1)
                last.then_inc(y_done if f == PAIRS - 1 else out_done, 1)

            def body(st):
                for f in range(PAIRS):
                    if st.has(0):
                        expand(st, f)
                    if f == 0 and st.has(-1):
                        contract(st, -1, PAIRS - 1)
                    if f > 0 and st.has(0):
                        contract(st, 0, f - 1)
                    if f == 1 and st.has(1):
                        transpose_x(st)

            run(pe, body)

        def g_free(eng, st, f):
            if f >= 2:
                eng.wait_ge(out_done, st.at(0) * (PAIRS - 1) + f - 1)
            elif st.has(-1):
                eng.wait_ge(*((out_done, st.at(0) * (PAIRS - 1)) if f == 0 else (y_done, st.done(-1))))

        @block.scalar
        def _(act):
            act.wait_ge(loaded, 8 * 16)

            def body(st):
                for f in range(PAIRS):
                    if st.has(0):
                        n = st.at(0) * PAIRS + f
                        act.wait_ge(z_done, 2 * n + 1)
                        if f >= 2 or st.has(-1):
                            act.wait_ge(g_ready, n - 1)
                        nc.scalar.activation(z0[f % 2][:], z_ps[f % 2][0][:], ACT.Relu).then_inc(z0_ready, 1)
                        act.wait_ge(g_ready, n + 1)
                        g_free(act, st, f)
                        nc.scalar.activation(g_hi[f % 2][:].rearrange("p j s -> p (j s)"), g_full[f % 2][:],
                                             ACT.Identity).then_inc(ghi_ready, 1)
                    if f == 2 and st.has(1):
                        p = st.parity(1)
                        act.wait_ge(xT_done, st.done(1))
                        if st.has(-1):
                            act.wait_ge(z_done, st.done(-1) * 2 * PAIRS)
                        nc.scalar.activation(x_hi[p][:].rearrange("p k s -> p (k s)"), xT_ps[:],
                                             ACT.Identity).then_inc(xhi_ready, 1)

            run(act, body)

        @block.vector
        def _(dve):
            dve.wait_ge(loaded, 8 * 16)
            for k in range(2):
                dve.tensor_tensor(sel[:, k:k + 1], row_expert[:], idx[:, k:k + 1],
                                  ALU.is_equal).then_inc(sel_ready, 1)
            dve.wait_ge(sel_ready, 2)
            for k in range(2):
                dve.tensor_scalar(b_sel[k][:], b_in[:], sel[:, k:k + 1], None, ALU.mult).then_inc(bsel_ready, 1)
            dve.tensor_copy(wo_hi[:], wo_in[:]).then_inc(w_ready, 1)
            for k in range(2):
                for d in range(KT):
                    for f in range(2):
                        cols = slice(f * 512, (f + 1) * 512)
                        dve.wait_ge(lora_done, 4 * k + 2 * d + f + 1)
                        dve.tensor_tensor(merged[k][:, d, cols], z_ps[d][f][:], w_in[:, d, cols],
                                          ALU.add).then_inc(merged_ready, 1)
                dve.wait_ge(merged_ready, 4 * k + 4)
                dve.tensor_copy(wm_hi[k][:], merged[k][:]).then_inc(w_ready, 1)

            def body(st):
                for f in range(PAIRS):
                    if st.has(0):
                        n = st.at(0) * PAIRS + f
                        dve.wait_ge(z_done, 2 * n + 2)
                        dve.tensor_scalar(z1[f % 2][:], z_ps[f % 2][1][:], 0.0, val[:, 1:2],
                                          ALU.max, ALU.mult).then_inc(z1_ready, 1)
                        dve.wait_ge(z1_ready, n + 1)
                        dve.wait_ge(z0_ready, n + 1)
                        if f >= 2 or st.has(-1):
                            dve.wait_ge(ghi_ready, n - 1)
                            dve.wait_ge(glo_ready, n - 1)
                        dve.scalar_tensor_tensor(g_full[f % 2][:], z0[f % 2][:], val[:, 0:1], z1[f % 2][:],
                                                 ALU.mult, ALU.add).then_inc(g_ready, 1)
                    if f == 2 and st.has(1):
                        p = st.parity(1)
                        dve.wait_ge(xhi_ready, st.done(1))
                        if st.has(-1):
                            dve.wait_ge(z_done, st.done(-1) * 2 * PAIRS)
                        dve.tensor_tensor(x_lo[p][:].rearrange("p k s -> p (k s)"), xT_ps[:],
                                          x_hi[p][:].bitcast(F32).rearrange("p k s -> p (k s)"),
                                          ALU.subtract).then_inc(xlo_ready, 1)
                    if f == 0 and st.has(-1):
                        norm.residual(dve, st, -1, [y[:, 0:D] for y in y_ps])
                    if f == 3 and st.has(-1):
                        norm.finish(dve, st, -1)

            run(dve, body)

        @block.gpsimd
        def _(pool):
            norm.constants(pool)
            for n, (lo, full, hi) in enumerate(((wo_lo, wo_in, wo_hi), (wm_lo[0], merged[0], wm_hi[0]),
                                                (wm_lo[1], merged[1], wm_hi[1]))):
                pool.wait_ge(w_ready, n + 1)
                pool.tensor_tensor(lo[:], full[:], hi[:].bitcast(F32), ALU.subtract).then_inc(lo_ready, 1)

            def body(st):
                for f in range(PAIRS):
                    if st.has(0):
                        n = st.at(0) * PAIRS + f
                        pool.wait_ge(ghi_ready, n + 1)
                        g_free(pool, st, f)
                        pool.tensor_tensor(g_lo[f % 2][:].rearrange("p j s -> p (j s)"), g_full[f % 2][:],
                                           g_hi[f % 2][:].bitcast(F32).rearrange("p j s -> p (j s)"),
                                           ALU.subtract).then_inc(glo_ready, 1)
                    if f == 0 and st.has(-1):
                        norm.inverse_root(pool, st, -1)

            run(pool, body)


def decoder(nc, a, out):
    rows = B * S
    mid = [nc.dram_tensor(f"mid{i}", (rows, D), F32, kind="Internal").ap() for i in range(5)]
    x_tiles = nc.dram_tensor("x_tiles", (ALL_TILES * TILE, D), F32, kind="Internal").ap()
    with ExitStack() as stack:
        slots_filled = stack.enter_context(nc.semaphore("slots_filled"))
        swdge = [stack.enter_context(nc.semaphore(f"swdge_{n}"))
                 for n in ("weights", "scattered", "gathered0", "gathered1")]
        with nc.Block() as block:
            @block.sync
            def _(sp):
                slots = x_tiles[SHARED_HALF * TILE:(SHARED_HALF + ROUTED) * TILE, :]
                sp.dma_start(slots, a["zeros"][0].partition_broadcast(ROUTED * TILE)).then_inc(slots_filled, 16)
        self_attention(nc, "self", a["x"], mid[0], a["self_w"], a["self_wo"], a["lambdas"], a["coef_parts"],
                       LAMBDA_INIT, a)
        cross_attention(nc, "cross", mid[0], mid[1], a["ctx_t"], a["cross0_w"], a["cross0_b"], None, a, False)
        mixture_of_experts(nc, "moe", mid[1], mid[2], x_tiles, slots_filled, swdge, a["router"], a["router_bias"],
                           a["experts"], a["moe_tables"], a)
        state_space(nc, "ssm", mid[2], mid[3], a["ssm_w"], a["conv_w"], a["conv_b"], a["norm_w"], a["ssm_wo"],
                    a["dt_bias"], a["a_log"], a["d_cols"], a["tri"], a)
        cross_attention(nc, "causal", mid[3], mid[4], a["ctx_t"], a["cross1_w"], a["cross1_b"], a["cross1_cols"], a, True)
        lora_feed_forward(nc, "ffn", mid[4], out, a["wi"], a["wo"], a["lora_a"], a["lora_b"], a["top_idx"],
                          a["top_val"], a["expert_of_row"], a)


def layout(inputs):
    g = {k: np.asarray(v) for k, v in inputs.items()}

    def kmajor(w):
        return w.reshape(-1, P, w.shape[1]).transpose(1, 0, 2)

    def columns(v):
        return v.reshape(-1, P).T

    def expert(gate, up, down):
        return np.concatenate([kmajor(w.T).reshape(P, -1) for w in (gate, up, down)], axis=1)

    i = np.arange(P)
    a = {}
    a["x"] = g["x"].reshape(B * S, D)
    a["ctx_t"] = g["ctx_1024"].transpose(0, 2, 1)
    a["zeros"] = np.zeros((1, D), np.float32)
    a["ident"] = np.eye(P, dtype=np.float32)
    a["identb"] = np.eye(P).astype(mybir.dt.np(BF16))
    masked = np.where(i[:, None] > i[None, :], MASKED, 0.0)
    a["mask"] = np.stack([masked, masked.T], 1).astype(mybir.dt.np(BF16))
    a["ones"] = np.broadcast_to(np.repeat(np.eye(2), HD, axis=1), (P, 2, 2 * HD)).astype(np.float32)
    upto = (i[:, None] <= i[None, :]).astype(np.float32)
    one = np.ones((P, P), np.float32)
    a["tri"] = np.stack([upto, one, upto, 1 - upto, one], 1)

    w_proj = g["L0_attn_Wproj"]
    quad, pair, feature = i // 32, (i % 32) // HD, i % HD
    a["self_w"] = kmajor(g["L0_attn_Wqkv"])
    a["self_wo"] = np.stack([w_proj[(4 * t + quad) * HD + feature] for t in range(4)]
                            + [w_proj[P * q + i] for q in range(QT)], 1)
    a["lambdas"] = np.stack([g["L0_attn_lambda_" + n] for n in ("q1", "k1", "q2", "k2")])
    a["coef_parts"] = np.stack([(1 - LAMBDA_INIT) * (pair == 0), -(1 - LAMBDA_INIT) * (pair == 1)],
                               1).astype(np.float32)

    a["cross0_w"] = np.stack([kmajor(g["L0_xattn_w_" + n].T) for n in "qkvo"], 1)
    b_o = g["L0_xattn_b_o"]
    a["cross0_b"] = np.stack([np.zeros_like(b_o), b_o])
    a["cross1_w"] = np.stack([kmajor(g["L1_xattn_W" + n].T) for n in "qkvo"], 1)
    a["cross1_b"] = np.stack([g["L1_xattn_bv"], g["L1_xattn_bo"]])
    a["cross1_cols"] = np.concatenate([columns(g["L1_xattn_bq"]), columns(g["L1_xattn_bk"])], 1)

    a["router"] = kmajor(g["L0_ffn_router_w"].T)
    a["router_bias"] = g["L0_ffn_routing_bias"]
    a["experts"] = np.concatenate([expert(g["L0_ffn_sg_w"], g["L0_ffn_su_w"], g["L0_ffn_sd_w"])]
                                  + [expert(g["L0_ffn_wg"][e], g["L0_ffn_wu"][e], g["L0_ffn_wd"][e])
                                     for e in range(NE)], 0)
    tables = np.zeros((P, 4 * P), np.float32)
    tables[:, 0:P] = i[:, None] < i[None, :]
    tables[:, P:2 * P] = 1
    tables[:, 2 * P:2 * P + NE] = NE - np.arange(NE)
    tables[:, 2 * P + NE:2 * P + 2 * NE] = TILE * np.arange(NE)
    tables[:, 2 * P + 2 * NE:2 * P + 2 * NE + ROUTED] = np.arange(ROUTED)
    tables[:, 3 * P] = i
    a["moe_tables"] = tables

    a["ssm_w"] = kmajor(g["L1_attn_in_proj_w"].T)
    a["conv_w"] = g["L1_attn_conv_w"].reshape(-1, P, 4).transpose(1, 0, 2)
    a["conv_b"] = columns(g["L1_attn_conv_b"])
    a["norm_w"] = columns(g["L1_attn_norm_w"])
    a["ssm_wo"] = kmajor(g["L1_attn_out_proj_w"].T)
    a["dt_bias"], a["a_log"] = g["L1_attn_dt_bias"], g["L1_attn_A_log"]
    a["d_cols"] = columns(np.repeat(g["L1_attn_D_param"], 64))

    a["wi"] = kmajor(g["L1_ffn_wi_w"].T)
    a["wo"] = kmajor(g["L1_ffn_wo_w"].T)
    a["lora_a"] = g["L1_ffn_lora_As"].reshape(P, D)
    a["lora_b"] = g["L1_ffn_lora_Bs"].transpose(0, 2, 1).reshape(P, -1)
    a["top_idx"], a["top_val"] = g["L1_ffn_top_k_indices"], g["L1_ffn_top_k_values"]
    a["expert_of_row"] = (i // 16).astype(np.float32)[:, None]
    return {k: np.ascontiguousarray(v) for k, v in a.items()}


def kernel(**inputs):
    import concourse.bacc as _bacc
    from concourse.bass_utils import run_bass_kernel_spmd as _run

    nc = _bacc.Bacc("TRN2", target_bir_lowering=False, num_devices=1)
    arrays = layout(inputs)
    aps = {k: nc.dram_tensor(k, v.shape, mybir.dt.from_np(v.dtype), kind="ExternalInput").ap()
           for k, v in arrays.items()}
    out = nc.dram_tensor("out", (B * S, D), F32, kind="ExternalOutput").ap()
    decoder(nc, aps, out)
    r = _run(nc, [arrays], core_ids=[0])
    return r.results[0]["out"].reshape(B, S, D)
```
